# Optimizing a Trainium2 kernel written in Bass

```python
import numpy as np
import jax
import jax.numpy as jnp

def _softmax(x, axis=-1):
    return jax.nn.softmax(x, axis=axis)

def _gelu(x):
    return jax.nn.gelu(x, approximate=True)

def _silu(x):
    return jax.nn.silu(x)

def _sigmoid(x):
    return jax.nn.sigmoid(x)

def _layernorm(x, axis=-1, eps=1e-05):
    m = jnp.mean(x, axis=axis, keepdims=True)
    v = jnp.var(x, axis=axis, keepdims=True)
    return (x - m) / jnp.sqrt(v + eps)

def _scatter_add(tgt, idx, src, axis=0):
    return tgt.at[idx].add(src)

def _segment_sum(src, seg, n):
    return jax.ops.segment_sum(src, seg, n)
kernel_name = 'mk_adj_ffn_d1_adj_r2_b4e8ac'

def setup_inputs(seed: int=0):
    np.random.seed(seed)
    _w = jnp.asarray

    def _rec_inputs():
        import jax
        import jax.numpy as jnp
        _gk = jax.random.key(seed)
        x = 7.22e-05 + 1 * jax.random.normal(jax.random.fold_in(_gk, 1), (128, 64, 128), jnp.float32)
        _a = jax.random.bernoulli(jax.random.fold_in(_gk, 2), 0.0625, (128, 64, 64))
        _a = jnp.logical_or(_a, jnp.swapaxes(_a, -1, -2))
        _a = jnp.logical_or(_a, jnp.eye(64, dtype=bool))
        _af = _a.astype(jnp.float32)
        _af = _af * jax.random.uniform(jax.random.fold_in(_gk, 3), (128, 64, 64), jnp.float32, 0.05, 1)
        adj = _af
        return (x, adj)
    x, adj = _rec_inputs()

    def _L0_gnn_setup():
        import jax, jax.numpy as jnp
        import numpy as np
        B, K, H = (32, 512, 128)
        LN_EPS = 1e-05

        def layer_norm(x, gamma, beta):
            mu = jnp.mean(x, axis=-1, keepdims=True)
            var = jnp.mean(jnp.square(x - mu), axis=-1, keepdims=True)
            return (x - mu) * jax.lax.rsqrt(var + LN_EPS) * gamma + beta
        key = jax.random.key(seed)
        k1, k2, k3, k4 = jax.random.split(key, 4)
        x = jax.random.normal(k1, (B, K, H), dtype=jnp.float32)
        adj = jax.random.uniform(k2, (B, K, K), dtype=jnp.float32)
        s = 1.0 / np.sqrt(H)
        W_rel = jax.random.normal(k3, (H, H), dtype=jnp.float32) * s
        b_rel = jnp.zeros((H,), dtype=jnp.float32)
        W_root = jax.random.normal(k4, (H, H), dtype=jnp.float32) * s
        ln_gamma = jnp.ones((H,), dtype=jnp.float32)
        ln_beta = jnp.zeros((H,), dtype=jnp.float32)
        return {'x': x, 'adj': adj, 'W_rel': W_rel, 'b_rel': b_rel, 'W_root': W_root, 'ln_gamma': ln_gamma, 'ln_beta': ln_beta}
    _L0_gnn_all = _L0_gnn_setup()
    _L0_gnn_in = {k: v for k, v in _L0_gnn_all.items() if k in ('W_rel', 'b_rel', 'W_root', 'ln_gamma', 'ln_beta')}
    del _L0_gnn_all

    def _L0_ffn_setup():
        import jax, jax.numpy as jnp
        import numpy as np
        B, S, D, H, E, K = (8, 4096, 128, 512, 8, 2)
        key = jax.random.key(seed)
        ks = jax.random.split(key, 7)
        s_in = 1.0 / np.sqrt(D)
        s_hid = 1.0 / np.sqrt(H)
        return {'x': jax.random.normal(ks[0], (B, S, D), dtype=jnp.float32), 'Wg': jax.random.uniform(ks[1], (E, D), jnp.float32, -s_in, s_in), 'bg': jax.random.uniform(ks[2], (E,), jnp.float32, -s_in, s_in), 'W1': jax.random.uniform(ks[3], (E, H, D), jnp.float32, -s_in, s_in), 'b1': jax.random.uniform(ks[4], (E, H), jnp.float32, -s_in, s_in), 'W2': jax.random.uniform(ks[5], (E, D, H), jnp.float32, -s_hid, s_hid), 'b2': jax.random.uniform(ks[6], (E, D), jnp.float32, -s_hid, s_hid)}
    _L0_ffn_all = _L0_ffn_setup()
    _L0_ffn_in = {k: v for k, v in _L0_ffn_all.items() if k in ('Wg', 'bg', 'W1', 'b1', 'W2', 'b2')}
    del _L0_ffn_all
    return {'x': x, 'adj': adj, 'L0_gnn_W_rel': _L0_gnn_in['W_rel'], 'L0_gnn_b_rel': _L0_gnn_in['b_rel'], 'L0_gnn_W_root': _L0_gnn_in['W_root'], 'L0_gnn_ln_gamma': _L0_gnn_in['ln_gamma'], 'L0_gnn_ln_beta': _L0_gnn_in['ln_beta'], 'L0_ffn_Wg': _L0_ffn_in['Wg'], 'L0_ffn_bg': _L0_ffn_in['bg'], 'L0_ffn_W1': _L0_ffn_in['W1'], 'L0_ffn_b1': _L0_ffn_in['b1'], 'L0_ffn_W2': _L0_ffn_in['W2'], 'L0_ffn_b2': _L0_ffn_in['b2']}

def reference(x, adj, L0_gnn_W_rel, L0_gnn_b_rel, L0_gnn_W_root, L0_gnn_ln_gamma, L0_gnn_ln_beta, L0_ffn_Wg, L0_ffn_bg, L0_ffn_W1, L0_ffn_b1, L0_ffn_W2, L0_ffn_b2):
    import jax
    import jax.numpy as jnp

    def _L0_gnn_ref(x, adj, W_rel, b_rel, W_root, ln_gamma, ln_beta):
        import jax, jax.numpy as jnp
        import numpy as np
        B, K, H = (32, 512, 128)
        LN_EPS = 1e-05

        def layer_norm(x, gamma, beta):
            mu = jnp.mean(x, axis=-1, keepdims=True)
            var = jnp.mean(jnp.square(x - mu), axis=-1, keepdims=True)
            return (x - mu) * jax.lax.rsqrt(var + LN_EPS) * gamma + beta
        h = layer_norm(x, ln_gamma, ln_beta)
        agg = jnp.einsum('bij,bjh->bih', adj, h)
        conv = jnp.einsum('bkh,ho->bko', agg, W_rel) + b_rel + jnp.einsum('bkh,ho->bko', h, W_root)
        return x + jax.nn.relu(conv)

    def _L0_ffn_ref(x, Wg, bg, W1, b1, W2, b2):
        import jax, jax.numpy as jnp
        import numpy as np
        B, S, D, H, E, K = (8, 4096, 128, 512, 8, 2)
        gate_scores = jnp.einsum('bsd,ed->bse', x, Wg) + bg
        topk_scores, topk_idx = jax.lax.top_k(gate_scores, K)
        topk_probs = jax.nn.softmax(topk_scores, axis=-1)
        combine = jnp.sum(topk_probs[..., None] * jax.nn.one_hot(topk_idx, E, dtype=x.dtype), axis=-2)
        out = jnp.zeros_like(x)
        for e in range(E):
            h = jax.nn.relu(jnp.einsum('bsd,hd->bsh', x, W1[e]) + b1[e])
            y = jnp.einsum('bsh,dh->bsd', h, W2[e]) + b2[e]
            out = out + combine[..., e:e + 1] * y
        return out
    x = x + _L0_gnn_ref(_layernorm(x, axis=-1), adj, L0_gnn_W_rel, L0_gnn_b_rel, L0_gnn_W_root, L0_gnn_ln_gamma, L0_gnn_ln_beta)
    x = x + _L0_ffn_ref(_layernorm(x, axis=-1), L0_ffn_Wg, L0_ffn_bg, L0_ffn_W1, L0_ffn_b1, L0_ffn_W2, L0_ffn_b2)
    return x

_drawn_inputs = setup_inputs


def setup_inputs(seed=0):
    import zlib

    import numpy as np

    out = dict(_drawn_inputs(seed))
    spreads = {'L0_gnn_b_rel': (0.0, 0.1), 'L0_gnn_ln_gamma': (1.0, 0.2), 'L0_gnn_ln_beta': (0.0, 0.1)}
    factors = {'L0_ffn_bg': 3.538, 'L0_ffn_b1': 8.0, 'L0_ffn_b2': 7.515}
    for name, (base, spread) in spreads.items():
        noise = np.random.default_rng([zlib.crc32(name.encode()), seed]).standard_normal(out[name].shape)
        drawn = base * np.exp(spread * noise) if base else spread * noise
        out[name] = jnp.asarray(drawn.astype(out[name].dtype))
    for name, factor in factors.items():
        out[name] = (out[name] * factor).astype(out[name].dtype)
    return out
```

```python
import concourse.bass as bass
import concourse.mybir as mybir
from contextlib import ExitStack

F32 = mybir.dt.float32
F16 = mybir.dt.float16
I32 = mybir.dt.int32
ACT = mybir.ActivationFunctionType
ALU = mybir.AluOpType
AXX = mybir.AxisListType.X

P = 128
E = 8
HID = 512
C = HID // P
TILES = 64
Q = 4
TQ = TILES // Q
GT = 4
NG = TQ // GT
NB = 2 * TQ + E
SB = NB // NG
LB = SB // 2
GW = GT * P
EPS = 1e-5
XS = 4.0
W1S = 32.0
W2S = 64.0
HS = XS * W1S
YS = HS * W2S
NEG = -3.0e38

K_ID, K_ONE, K_BREL, K_BG, K_DESC, K_B128, K_GAM, K_BET, K_END = (
    0, 128, 256, 768, 800, 808, 848, 849, 850)
H_ID, H_TRI, H_ONE, H_B1M, H_B2M, H_END = 0, 128, 256, 384, 896, 1024


def build(nc, x, adj, wrel, wroot, wg, w1, w2, b1, b2, kf, kh, out):
    ctx = ExitStack()
    with ctx:
        def sb(name, shape, dt=F32):
            return ctx.enter_context(nc.sbuf_tensor(name, shape, dt))

        def pb(name, dt=F32):
            return ctx.enter_context(nc.psum_tensor(name, [P, 512 if dt == F32 else 1024], dt))

        def sem(name):
            return ctx.enter_context(nc.semaphore(name))


        rows = [nc.dram_tensor(f"rows{q}", [P * NB, P], F32, kind="Internal").ap() for q in range(Q)]
        yrows = [nc.dram_tensor(f"yrows{q}", [P * NB, P], F32, kind="Internal").ap() for q in range(Q)]
        rows_p = [r.rearrange("(p b) d -> p (b d)", p=P) for r in rows]
        yrows_p = [r.rearrange("(p b) d -> p (b d)", p=P) for r in yrows]

        KF = sb("KF", [P, K_END])
        KH = sb("KH", [P, H_END], F16)
        WREL = sb("WREL", [P, P])
        WROOT = sb("WROOT", [P, P])
        WG = sb("WG", [P, E])
        X = sb("X", [P, TILES * P])
        ADJ = sb("ADJ", [P, GW])
        STAGE = sb("STAGE", [P, E * HID])
        W1H = sb("W1H", [P, E * HID], F16)
        W1L = sb("W1L", [P, E * HID], F16)
        W2H = sb("W2H", [P, E * HID], F16)
        W2L = sb("W2L", [P, E * HID], F16)
        B1 = sb("B1", [P, E * P], F16)
        B2 = sb("B2", [P, E * P], F16)
        B12 = sb("B12", [64, 2 * E * P])
        BT = sb("BT", [64, 2 * E * P], F16)
        H0 = sb("H0", [P, GW])
        HT = sb("HT", [P, GW])
        U = sb("U", [P, GW])
        TMP = sb("TMP", [P, GW])
        XN = sb("XN", [P, GW])
        XNT = sb("XNT", [P, GW])
        ST = sb("ST", [P, GT * 6])
        MEAN2, MDIF, VARN = sb("MEAN2", [P, GT]), sb("MDIF", [P, GT]), sb("VARN", [P, GT])
        IDLE = sb("IDLE", [P, 1])
        RA = sb("RA", [P, 2 * GT])
        RR = sb("RR", [P, 2 * GT])
        RT = sb("RT", [P, 2 * GT])
        NBI = sb("NBI", [P, 2 * GT])
        R1P = sb("R1P", [P, GT])
        XHL = sb("XHL", [P, 2 * TQ * 2 * P], F16)
        LG = sb("LG", [P, TQ * E])
        M1 = sb("M1", [P, TQ])
        M2 = sb("M2", [P, TQ])
        KM = sb("KM", [P, TQ])
        EQ = sb("EQ", [P, TQ * E])
        OH = sb("OH", [P, 2 * TQ * E])
        LG2 = sb("LG2", [P, TQ * E])
        DM = sb("DM", [P, TQ])
        EX = sb("EX", [P, TQ])
        DEN = sb("DEN", [P, TQ])
        PR = sb("PR", [P, Q * 2 * TQ])
        MK = sb("MK", [P, E * TQ], F16)
        TOT = sb("TOT", [P, E * TQ])
        SC = sb("SC", [P, E * TQ])
        POS = sb("POS", [P, E * TQ])
        CNT = sb("CNT", [P, E])
        CNI = sb("CNI", [P, E], I32)
        PADI = sb("PADI", [P, E], I32)
        PADF = sb("PADF", [P, E])
        PEND = sb("PEND", [P, E])
        SHF = sb("SHF", [P, E])
        SLF = sb("SLF", [P, 2 * TQ])
        SLI = sb("SLI", [P, 2 * TQ], I32)
        SLA = sb("SLA", [P, 2 * TQ], I32)
        SLB = sb("SLB", [P, 2 * TQ], I32)
        SLC = sb("SLC", [P, 2 * TQ], I32)
        IDX = sb("IDX", [P, Q * 2 * TQ], I32)
        BEF = sb("BEF", [1, NB * (E - 1)])
        BES = sb("BES", [1, NB])
        BEI = sb("BEI", [1, Q * NB], I32)
        XB = sb("XB", [P, SB * P])
        XT = sb("XT", [P, 2 * 2 * P], F16)
        HH = sb("HH", [P, 2 * HID], F16)
        HL = sb("HL", [P, 2 * HID], F16)
        YB = sb("YB", [P, SB * P])
        YG = [STAGE, sb("YG1", [P, 2 * TQ * P])]

        PH = [pb("PH0"), pb("PH1")]
        PX = [pb("PX0", F16), pb("PX1", F16)]
        PY = [pb("PY0"), pb("PY1")]
        PA, PB = pb("PA"), pb("PB")

        const_in = sem("const_in")
        x_in = [sem(f"x_in{q}") for q in range(Q)]
        adj_zero, adj_in = sem("adj_zero"), sem("adj_in")
        w1_in, w2_in, b_in = sem("w1_in"), sem("w2_in"), sem("b_in")
        zero_made = sem("zero_made")
        zero_out = [sem(f"zero_out{q}") for q in range(Q)]
        whi_made, wlo_made, bhi_made, bt_made, bias_made, bias_zero = (
            sem("whi_made"), sem("wlo_made"), sem("bhi_made"), sem("bt_made"), sem("bias_made"), sem("bias_zero"))
        dve_step = sem("dve_step")
        h0_made, h0T_done, hT_made = sem("h0_made"), sem("h0T_done"), sem("hT_made")
        u_done, u_made, conv_done = sem("u_done"), sem("u_made"), sem("conv_done")
        xn_made, xhi_made, xlo_made = sem("xn_made"), sem("xhi_made"), sem("xlo_made")
        xnT_done, xnT_made, score_done, score_made = (
            sem("xnT_done"), sem("xnT_made"), sem("score_done"), sem("score_made"))
        gap_made, ex_made, mask_made, rank_done = sem("gap_made"), sem("ex_made"), sem("mask_made"), sem("rank_done")
        rank_used, slots_made, experts_made = sem("rank_used"), sem("slots_made"), sem("experts_made")
        scattered = [sem(f"scattered{q}") for q in range(Q)]
        xb_in = [sem("xb_in0"), sem("xb_in1")]
        xT_done, xT_made = sem("xT_done"), sem("xT_made")
        h_done, hi_made, lo_made = sem("h_done"), sem("hi_made"), sem("lo_made")
        y_done, y_made = sem("y_done"), sem("y_made")
        y_out = [sem("y_out0"), sem("y_out1")]
        gathered = [sem(f"gathered{q}") for q in range(Q)]
        combined, out_done = sem("combined"), sem("out_done")

        block = ctx.enter_context(nc.Block())

        def cols(t, start, size):
            return t[:, bass.ds(start, size)]

        def hi_lo(q, i):
            v = cols(XHL, (q % 2 * TQ + i * GT) * 2 * P, 2 * GW).rearrange("p (t s d) -> p s t d", s=2, d=P)
            return v[:, 0], v[:, 1]

        @block.sync
        def _(sp):
            sp.sem_inc(y_out[0], 16)
            sp.sem_inc(y_out[1], 16)
            sp.dma_start(X[:, 0:TQ * P], x[:, 0:TQ * P]).then_inc(x_in[0], 16)
            sp.dma_start(KF[:, :], kf[:, :]).then_inc(const_in, 16)
            sp.dma_start(KH[:, :], kh[:, :]).then_inc(const_in, 16)
            sp.dma_start(WREL[:, :], wrel[:, :]).then_inc(const_in, 16)
            sp.dma_start(WROOT[:, :], wroot[:, :]).then_inc(const_in, 16)
            sp.dma_start(WG[:, :], wg[:, :]).then_inc(const_in, 16)

            def load_adj(g):
                d = ADJ[:, :].rearrange("p (t c) -> p t c", c=P)
                s = adj[:, bass.ds(g * (GT * 64), GT * 64)].rearrange("p (t c) -> p t c", c=64)
                sp.dma_start(d[0:64, :, 0:64], s[0:64]).then_inc(adj_in, 16)
                sp.dma_start(d[64:P, :, 64:P], s[64:P]).then_inc(adj_in, 16)

            sp.wait_ge(adj_zero, 1)
            load_adj(0)
            with sp.Fori(1, 2 * NG) as g:
                sp.wait_ge(conv_done, g)
                load_adj(g)

            def load_rows(q, c, j):
                sp.dma_start(XB[:, j * LB * P:(j + 1) * LB * P], rows_p[q][:, bass.ds(c * (LB * P), LB * P)]).then_inc(xb_in[j], 16)

            def store_y(q, i, j):
                sp.wait_ge(y_made, q * NB + i * SB + (j + 1) * LB + 2)
                sp.dma_start(yrows_p[q][:, bass.ds((2 * i + j) * (LB * P), LB * P)],
                             YB[:, j * LB * P:(j + 1) * LB * P]).then_inc(y_out[j], 16)

            sp.wait_ge(scattered[0], 2 * TQ * 16)
            for j in range(2):
                load_rows(0, j, j)
            for q in range(Q):
                def chunk_pair(i, last):
                    if q + 2 < Q:
                        sp.wait_ge(conv_done, (q + 2) * NG + i)
                        load_adj((q + 2) * NG + i)
                    for j in range(2):
                        if not (last and q == Q - 1):
                            sp.wait_ge(xT_done, q * NB + i * SB + (j + 1) * LB)
                            if last:
                                if j == 0:
                                    sp.wait_ge(scattered[q + 1], 2 * TQ * 16)
                                load_rows(q + 1, j, j)
                            else:
                                load_rows(q, 2 * i + 2 + j, j)
                        store_y(q, i, j)
                with sp.Fori(0, NG - 1) as i:
                    chunk_pair(i, False)
                chunk_pair(NG - 1, True)

            with sp.Fori(0, Q * NG) as g:
                sp.wait_ge(combined, g + 1)
                sp.dma_start(out[:, bass.ds(g * GW, GW)], cols(X, g * GW, GW)).then_inc(out_done, 16)
            sp.wait_ge(out_done, Q * NG * 16)

        @block.gpsimd
        def _(pool):
            nc.gpsimd.memset(ADJ[:, :], 0.0).then_inc(adj_zero, 1)
            nc.gpsimd.memset(YG[1][:, 0:NB * P // 2], 0.0).then_inc(zero_made, 1)
            nc.gpsimd.memset(B1[:, :], 0.0).then_inc(bias_zero, 1)
            nc.gpsimd.memset(B2[:, :], 0.0).then_inc(bias_zero, 1)

            def scatter(q):
                pool.wait_ge(slots_made, q + 1)
                pool.wait_ge(xlo_made, (q + 1) * NG)
                pool.wait_ge(zero_out[q], 32)
                for t in range(TQ):
                    for k in range(2):
                        col = (q * 2 + k) * TQ + t
                        src = (q % 2 * TQ + t) * 2 * P
                        nc.gpsimd.indirect_dma_start(
                            rows[q], bass.IndirectOffsetOnAxis(ap=IDX[:, col:col + 1], axis=0),
                            XHL[:, src:src + 2 * P].bitcast(F32), None).then_inc(scattered[q], 16)

            def gather(q):
                for j in range(2):
                    pool.wait_ge(y_out[j], 16 + (q + 1) * 16 * NG)
                if q >= 2:
                    pool.wait_ge(combined, (q - 1) * NG)
                for t in range(TQ):
                    for k in range(2):
                        col = (q * 2 + k) * TQ + t
                        dst = (t * 2 + k) * P
                        nc.gpsimd.indirect_dma_start(
                            YG[q % 2][:, dst:dst + P], None, yrows[q],
                            bass.IndirectOffsetOnAxis(ap=IDX[:, col:col + 1], axis=0)).then_inc(gathered[q], 16)

            scatter(0)
            scatter(1)
            scatter(2)
            gather(0)
            scatter(3)
            gather(1)
            gather(2)
            gather(3)
            for q in range(Q):
                pool.wait_ge(gathered[q], 2 * TQ * 16)

        @block.vector
        def _(dve):
            seq = [0, 0]

            def step(ins):
                ins.then_inc(dve_step, 1)
                seq[1] += 1

            def settle():
                dve.wait_ge(dve_step, seq[0] + seq[1])

            def loop(n, steps, body):
                before = seq[0] + seq[1]
                with dve.Fori(0, n) as i:
                    seq[0], seq[1] = before + i * steps, 0
                    body(i)
                    assert seq[1] == steps, (steps, seq[1])
                seq[0], seq[1] = before + n * steps, 0

            def rsqrt(n):
                a, r, t = RA[:, 0:n], RR[:, 0:n], RT[:, 0:n]
                step(nc.vector.tensor_scalar(t.bitcast(I32), a.bitcast(I32), 1, None, ALU.logical_shift_right)); settle()
                step(nc.vector.tensor_scalar(r.bitcast(I32), t.bitcast(I32), -1.0, float(0x5F3759DF), ALU.mult, ALU.add)); settle()
                for _ in range(3):
                    step(nc.vector.tensor_tensor(t, r, r, ALU.mult)); settle()
                    step(nc.vector.scalar_tensor_tensor(t, t, -0.5, a, ALU.mult, ALU.mult)); settle()
                    step(nc.vector.scalar_tensor_tensor(r, t, 1.5, r, ALU.add, ALU.mult)); settle()

            def stats(g):
                nc.vector.memset(IDLE[:, :], 0.0)
                for k in range(GT):
                    step(nc.vector.bn_stats(ST[:, 6 * k:6 * k + 6], cols(X, g * GW + k * P, P)))
                settle()
                half = ST[:, :].rearrange("p (k s) -> p s k", s=6)
                step(nc.vector.tensor_tensor(MEAN2[:, :], half[:, 1], half[:, 4], ALU.add))
                step(nc.vector.tensor_tensor(MDIF[:, :], half[:, 1], half[:, 4], ALU.subtract))
                step(nc.vector.tensor_tensor(VARN[:, :], half[:, 2], half[:, 5], ALU.add)); settle()
                step(nc.vector.tensor_tensor(MDIF[:, :], MDIF[:, :], MDIF[:, :], ALU.mult)); settle()
                step(nc.vector.scalar_tensor_tensor(VARN[:, :], MDIF[:, :], P / 4.0, VARN[:, :], ALU.mult, ALU.add)); settle()

            def stats_in(g):
                stats(g)
                step(nc.vector.tensor_scalar(RA[:, 0:GT], VARN[:, :], 1.0 / P, EPS, ALU.mult, ALU.add))
                step(nc.vector.tensor_scalar(RA[:, GT:2 * GT], VARN[:, :], (1.0 + EPS) / P, EPS * EPS, ALU.mult, ALU.add)); settle()

            def scales_in(g):
                rsqrt(2 * GT)
                for n in range(2):
                    step(nc.vector.scalar_tensor_tensor(NBI[:, n * GT:(n + 1) * GT], MEAN2[:, :], -0.5, RR[:, n * GT:(n + 1) * GT],
                                                        ALU.mult, ALU.mult))
                step(nc.vector.tensor_scalar(R1P[:, :], RR[:, 0:GT], 1.0, None, ALU.add)); settle()

            def norm_in(g):
                dve.wait_ge(h0T_done, g + 1)
                for k in range(GT):
                    last = nc.vector.tensor_scalar(H0[:, k * P:(k + 1) * P], cols(X, g * GW + k * P, P),
                                                   RR[:, GT + k:GT + k + 1], NBI[:, GT + k:GT + k + 1], ALU.mult, ALU.add)
                last.then_inc(h0_made, 1)
                for k in range(GT):
                    last = nc.vector.tensor_scalar(cols(X, g * GW + k * P, P), cols(X, g * GW + k * P, P),
                                                   R1P[:, k:k + 1], NBI[:, k:k + 1], ALU.mult, ALU.add)
                step(last)

            def residual(g):
                dve.wait_ge(conv_done, g + 1)
                step(nc.vector.tensor_tensor(TMP[:, :], PA[:, :], KF[:, K_BREL:K_BREL + GW], ALU.add)); settle()
                step(nc.vector.scalar_tensor_tensor(cols(X, g * GW, GW), TMP[:, :], 0.0, cols(X, g * GW, GW), ALU.max, ALU.add)); settle()
                stats(g)
                step(nc.vector.tensor_scalar(RA[:, 0:GT], VARN[:, :], 1.0 / P, EPS, ALU.mult, ALU.add)); settle()

            def scales_out(g):
                rsqrt(GT)
                step(nc.vector.scalar_tensor_tensor(NBI[:, 0:GT], MEAN2[:, :], -0.5, RR[:, 0:GT], ALU.mult, ALU.mult)); settle()

            def norm_out(g):
                dve.wait_ge(xnT_done, g + 1)
                dve.wait_ge(xhi_made, g + 1)
                for k in range(GT):
                    last = nc.vector.tensor_scalar(XN[:, k * P:(k + 1) * P], cols(X, g * GW + k * P, P),
                                                   RR[:, k:k + 1], NBI[:, k:k + 1], ALU.mult, ALU.add)
                last.then_inc(xn_made, 1)

            def split_low(q, i, g):
                dve.wait_ge(xhi_made, g + 2)
                hi, lo = hi_lo(q, i)
                nc.vector.scalar_tensor_tensor(lo, XN[:, :].rearrange("p (t d) -> p t d", d=P), XS, hi,
                                               ALU.mult, ALU.subtract).then_inc(xlo_made, 1)

            def scores(i, g):
                dve.wait_ge(score_done, g + 1)
                nc.vector.tensor_tensor(cols(LG, i * (GT * E), GT * E), PA[:, 0:GT * E], KF[:, K_BG:K_BG + GT * E],
                                        ALU.add).then_inc(score_made, 1)

            def te(ap):
                return ap.rearrange("p (t e) -> p t e", e=E)

            def per_tile(t):
                return t[:, :].unsqueeze(2).to_broadcast([P, TQ, E])

            ohs = [OH[:, k * TQ * E:(k + 1) * TQ * E] for k in range(2)]

            def one_hot(src, m, k):
                desc = KF[:, K_DESC:K_DESC + E].unsqueeze(1).to_broadcast([P, TQ, E])
                step(nc.vector.tensor_reduce(m[:, :], te(src[:, :]), AXX, ALU.max)); settle()
                step(nc.vector.tensor_tensor(te(EQ[:, :]), te(src[:, :]), per_tile(m), ALU.is_equal)); settle()
                step(nc.vector.tensor_tensor(te(EQ[:, :]), te(EQ[:, :]), desc, ALU.mult)); settle()
                step(nc.vector.tensor_reduce(KM[:, :], te(EQ[:, :]), AXX, ALU.max)); settle()
                step(nc.vector.tensor_tensor(te(ohs[k]), te(EQ[:, :]), per_tile(KM), ALU.is_equal)); settle()

            def route_top(q):
                dve.wait_ge(score_made, (q + 1) * NG + 1)
                one_hot(LG, M1, 0)
                step(nc.vector.scalar_tensor_tensor(LG2[:, :], ohs[0], NEG, LG[:, :], ALU.mult, ALU.add)); settle()
                one_hot(LG2, M2, 1)
                nc.vector.tensor_tensor(MK[:, :].rearrange("p (e t) -> p t e", t=TQ), te(ohs[0]), te(ohs[1]),
                                        ALU.add).then_inc(mask_made, 1)
                nc.vector.tensor_tensor(DM[:, :], M2[:, :], M1[:, :], ALU.subtract).then_inc(gap_made, 1)

            def et(t):
                return t[:, :].rearrange("p (e t) -> p e t", t=TQ)

            def route_slots(q):
                dve.wait_ge(rank_done, q + 1)
                step(nc.vector.tensor_copy(TOT[:, :], PB[:, 0:E * TQ])); settle()
                step(nc.vector.tensor_tensor_scan(SC[:, :], KF[:, K_ONE:K_ONE + E * TQ], TOT[:, :], 0.0, ALU.mult, ALU.add))
                step(nc.vector.tensor_reduce(CNT[:, :], et(TOT), AXX, ALU.add)); settle()
                step(nc.vector.tensor_tensor(POS[:, :], SC[:, :], TOT[:, :], ALU.subtract))
                step(nc.vector.tensor_scalar(CNI[:, :], CNT[:, :], float(P - 1), None, ALU.add)); settle()
                ins = nc.vector.tensor_tensor(POS[:, :], POS[:, :], PA[:, 0:E * TQ], ALU.add)
                step(ins)
                step(nc.vector.tensor_scalar(PADI[:, :], CNI[:, :], 7, 7, ALU.logical_shift_right, ALU.logical_shift_left)); settle()
                step(nc.vector.tensor_copy(PADF[:, :], PADI[:, :])); settle()
                step(nc.vector.tensor_tensor_scan(PEND[:, :], KF[:, K_ONE:K_ONE + E], PADF[:, :], 0.0, ALU.mult, ALU.add)); settle()
                step(nc.vector.tensor_tensor(SHF[:, :], PEND[:, :], PADF[:, :], ALU.subtract)); settle()
                step(nc.vector.tensor_tensor(SHF[:, :], SHF[:, :], CNT[:, :], ALU.add)); settle()
                step(nc.vector.tensor_tensor(SHF[:, :], SHF[:, :], et(SC)[:, :, TQ - 1], ALU.subtract)); settle()
                nc.vector.tensor_tensor(et(POS), et(POS), SHF[:, :].unsqueeze(2).to_broadcast([P, E, TQ]), ALU.add).then_inc(rank_used, 1)
                dve.wait_ge(rank_used, q + 1)
                for k in range(2):
                    step(nc.vector.tensor_tensor(te(EQ[:, :]), te(ohs[k]), POS[:, :].rearrange("p (e t) -> p t e", t=TQ), ALU.mult)); settle()
                    step(nc.vector.tensor_reduce(SLF[:, k * TQ:(k + 1) * TQ], te(EQ[:, :]), AXX, ALU.add)); settle()
                step(nc.vector.tensor_copy(SLI[:, :], SLF[:, :])); settle()
                step(nc.vector.tensor_scalar(SLA[:, :], SLI[:, :], P - 1, None, ALU.bitwise_and))
                step(nc.vector.tensor_scalar(SLB[:, :], SLI[:, :], 7, None, ALU.logical_shift_right)); settle()
                nc.vector.scalar_tensor_tensor(IDX[:, q * 2 * TQ:(q + 1) * 2 * TQ], SLA[:, :], float(NB), SLB[:, :],
                                               ALU.mult, ALU.add).then_inc(slots_made, 1)
                step(nc.vector.tensor_tensor(BEF[:, :].rearrange("p (b e) -> p b e", e=E - 1),
                                             KF[0:1, K_B128:K_B128 + NB].unsqueeze(2).to_broadcast([1, NB, E - 1]),
                                             PEND[0:1, 0:E - 1].unsqueeze(1).to_broadcast([1, NB, E - 1]), ALU.is_ge)); settle()
                step(nc.vector.tensor_reduce(BES[:, :], BEF[:, :].rearrange("p (b e) -> p b e", e=E - 1), AXX, ALU.add)); settle()
                nc.vector.tensor_scalar(BEI[:, q * NB:(q + 1) * NB], BES[:, :], float(P), None, ALU.mult).then_inc(experts_made, 1)
                p1 = PR[:, q * 2 * TQ:q * 2 * TQ + TQ]
                dve.wait_ge(ex_made, q + 1)
                step(nc.vector.tensor_scalar(DEN[:, :], EX[:, :], 1.0, None, ALU.add)); settle()
                step(nc.vector.reciprocal(p1, DEN[:, :])); settle()
                step(nc.vector.tensor_tensor(PR[:, q * 2 * TQ + TQ:(q + 1) * 2 * TQ], EX[:, :], p1, ALU.mult)); settle()

            def xT_copy(b, j):
                dve.wait_ge(xT_done, b + 1)
                dve.wait_ge(h_done, b + 1)
                nc.vector.tensor_copy(XT[:, j % 2 * 2 * P:(j % 2 + 1) * 2 * P], PX[j % 2][:, 0:2 * P]).then_inc(xT_made, 1)

            def low_half(b, j):
                dve.wait_ge(hi_made, b + 1)
                nc.vector.scalar_tensor_tensor(HL[:, j % 2 * HID:(j % 2 + 1) * HID], PH[j % 2][:, :], 0.0,
                                               HH[:, j % 2 * HID:(j % 2 + 1) * HID], ALU.max, ALU.subtract).then_inc(lo_made, 1)

            def combine(q, i, k):
                xv = cols(X, (q * NG + i) * GW + k * P, P)
                for e in range(2):
                    y = cols(YG[q % 2], (i * GT + k) * 2 * P + e * P, P)
                    ins = nc.vector.scalar_tensor_tensor(xv, y, cols(PR, (q * 2 + e) * TQ + i * GT + k, 1), xv, ALU.mult, ALU.add)
                    if e == 0:
                        step(ins)
                        settle()
                    elif k == GT - 1:
                        ins.then_inc(combined, 1)

            dve.sem_inc(xT_made, 2)
            dve.sem_inc(lo_made, 2)
            dve.sem_inc(score_made, 1)
            dve.wait_ge(const_in, 80)

            def graph_group(q):
                def body(i):
                    g = q * NG + i
                    stats_in(g)
                    scales_in(g)
                    norm_in(g)
                    residual(g)
                    scales_out(g)
                    norm_out(g)
                    split_low(q, i, g)
                    scores(i, g)
                return body

            PER_GROUP = (GT + 5 + 2) + (2 + 9 + 3) + 1 + (2 + GT + 5 + 1) + (2 + 9 + 1)
            dve.wait_ge(x_in[0], 16)
            loop(NG, PER_GROUP, graph_group(0))
            route_top(0)
            route_slots(0)
            dve.wait_ge(whi_made, 1)
            nc.vector.scalar_tensor_tensor(W1L[:, :], STAGE[:, :], W1S, W1H[:, :], ALU.mult, ALU.subtract).then_inc(wlo_made, 1)
            dve.wait_ge(bt_made, 2)
            for n, (dst, r, s) in enumerate(((B1, 4, HS), (B2, 1, YS / 64.0))):
                v = slice(n * E * P, (n + 1) * E * P)
                nc.vector.scalar_tensor_tensor(dst[32:32 + r, :], B12[32:32 + r, v], s, BT[32:32 + r, v],
                                               ALU.mult, ALU.subtract).then_inc(bias_made, 1)
            dve.wait_ge(x_in[1], 16)
            loop(NG, PER_GROUP, graph_group(1))
            route_top(1)
            route_slots(1)
            dve.wait_ge(whi_made, 2)
            nc.vector.scalar_tensor_tensor(W2L[:, :], STAGE[:, :], W2S, W2H[:, :], ALU.mult, ALU.subtract).then_inc(wlo_made, 1)

            xT_copy(0, 0)
            for q in range(Q):
                graph = q + 2 < Q
                if graph:
                    dve.wait_ge(x_in[q + 2], 16)
                else:
                    dve.wait_ge(gathered[q - 2], 2 * TQ * 16)

                def blocks_pass(i, last=False):
                    g = (q + 2) * NG + i
                    pieces = {0: lambda: stats_in(g), 1: lambda: scales_in(g), 2: lambda: norm_in(g),
                              6: lambda: residual(g), 7: lambda: (scales_out(g), norm_out(g)),
                              8: lambda: split_low(q, i, g), 9: lambda: scores(i, g)} if graph else {
                              2 * k: lambda k=k: combine(q - 2, i, k) for k in range(GT)}
                    for j in range(SB):
                        b = q * NB + i * SB + j
                        if not (last and j == SB - 1):
                            xT_copy(b + 1, j + 1)
                        low_half(b, j)
                        if j in pieces:
                            pieces[j]()
                n = NG - (q == Q - 1)
                loop(n, PER_GROUP if graph else GT, blocks_pass)
                if n < NG:
                    blocks_pass(n, True)
                if graph:
                    route_top(q + 2)
                    route_slots(q + 2)
            for q in range(Q - 2, Q):
                dve.wait_ge(gathered[q], 2 * TQ * 16)
                loop(NG, GT, lambda i: [combine(q, i, k) for k in range(GT)])

        @block.scalar
        def _(act):
            act.sem_inc(xhi_made, 1)
            act.sem_inc(y_made, 2)
            act.wait_ge(zero_made, 1)

            def zero_rows(q):
                for h in range(2):
                    w = NB * P // 2
                    act.dma_start(rows_p[q][:, h * w:(h + 1) * w], YG[1][:, 0:w]).then_inc(zero_out[q], 16)

            zero_rows(0)
            act.dma_start(STAGE[:, :], w1[:, :]).then_inc(w1_in, 16)
            act.dma_start(X[:, TQ * P:2 * TQ * P], x[:, TQ * P:2 * TQ * P]).then_inc(x_in[1], 16)
            for r in (0, 32):
                act.dma_start(B12[r:r + 4, 0:E * P], b1[:, :]).then_inc(b_in, 16)
                act.dma_start(B12[r:r + 1, E * P:2 * E * P], b2[:, :]).then_inc(b_in, 16)
            zero_rows(1)

            def hT_copy(g):
                act.wait_ge(h0T_done, g + 2)
                nc.scalar.activation(HT[:, :], PA[:, :], ACT.Identity, bias=KF[:, K_BET:K_BET + 1],
                                     scale=KF[:, K_GAM:K_GAM + 1]).then_inc(hT_made, 1)

            def u_copy(g):
                act.wait_ge(u_done, g + 1)
                nc.scalar.copy(U[:, :], PB[:, :]).then_inc(u_made, 1)

            def split_high(q, i, g):
                act.wait_ge(xn_made, g + 1)
                nc.scalar.activation(hi_lo(q, i)[0], XN[:, :].rearrange("p (t d) -> p t d", d=P), ACT.Copy,
                                     scale=XS).then_inc(xhi_made, 1)

            def xnT_copy(g):
                act.wait_ge(xnT_done, g + 2)
                nc.scalar.copy(XNT[:, :], PB[:, :]).then_inc(xnT_made, 1)

            def exp_gap(q):
                act.wait_ge(gap_made, q + 1)
                nc.scalar.activation(EX[:, :], DM[:, :], ACT.Exp).then_inc(ex_made, 1)

            def high_half(b, j):
                act.wait_ge(h_done, b + 3)
                act.wait_ge(y_done, b + 1)
                nc.scalar.activation(HH[:, j % 2 * HID:(j % 2 + 1) * HID], PH[j % 2][:, :], ACT.Relu).then_inc(hi_made, 1)

            def y_copy(b, j, stored):
                act.wait_ge(y_done, b + 3)
                if j % LB == 0:
                    act.wait_ge(y_out[j // LB], stored)
                nc.scalar.mul(YB[:, j * P:(j + 1) * P], PY[j % 2][:, 0:P], 1.0 / YS).then_inc(y_made, 1)

            act.wait_ge(const_in, 80)
            for q in range(2):
                with act.Fori(0, NG) as i:
                    g = q * NG + i
                    hT_copy(g)
                    u_copy(g)
                    split_high(q, i, g)
                    xnT_copy(g)
                exp_gap(q)
                if q == 0:
                    act.wait_ge(w1_in, 16)
                    nc.scalar.activation(W1H[:, :], STAGE[:, :], ACT.Copy, scale=W1S).then_inc(whi_made, 1)
                    act.wait_ge(bias_zero, 2)
                    act.wait_ge(b_in, 64)
                    for n, (dst, r, s) in enumerate(((B1, 4, HS), (B2, 1, YS / 64.0))):
                        v = slice(n * E * P, (n + 1) * E * P)
                        nc.scalar.activation(dst[0:r, :], B12[0:r, v], ACT.Copy, scale=s).then_inc(bias_made, 1)
                        nc.scalar.activation(BT[32:32 + r, v], B12[32:32 + r, v], ACT.Copy, scale=s).then_inc(bt_made, 1)
                    act.wait_ge(wlo_made, 1)
                    act.dma_start(STAGE[:, :], w2[:, :]).then_inc(w2_in, 16)
                    for r in range(2, Q):
                        act.dma_start(X[:, r * TQ * P:(r + 1) * TQ * P], x[:, r * TQ * P:(r + 1) * TQ * P]).then_inc(x_in[r], 16)
                        zero_rows(r)
            act.wait_ge(w2_in, 16)
            nc.scalar.activation(W2H[:, :], STAGE[:, :], ACT.Copy, scale=W2S).then_inc(whi_made, 1)
            for q in range(Q):
                graph = q + 2 < Q
                if graph:
                    act.wait_ge(scattered[q], 2 * TQ * 16)

                def blocks_pass(i, first=False):
                    g = (q + 2) * NG + i
                    pieces = {3: lambda: hT_copy(g), 4: lambda: u_copy(g), 8: lambda: split_high(q, i, g),
                              9: lambda: xnT_copy(g)} if graph else {}
                    for j in range(SB):
                        b = q * NB + i * SB + j
                        high_half(b, j)
                        if j > 0:
                            y_copy(b - 1, j - 1, (q * NG + i + 1) * 16)
                        elif not first:
                            y_copy(b - 1, SB - 1, None)
                        if j in pieces:
                            pieces[j]()
                n = 1 if q == 0 else 0
                if n:
                    blocks_pass(0, True)
                with act.Fori(n, NG) as i:
                    blocks_pass(i)
                if graph:
                    exp_gap(q + 2)
            y_copy(Q * NB - 1, SB - 1, None)

        @block.tensor
        def _(pe):
            ident, ident16 = KF[:, K_ID:K_ID + P], KH[:, H_ID:H_ID + P]
            for s in (h0T_done, xnT_done):
                pe.sem_inc(s, 1)
            for s in (h_done, y_done):
                pe.sem_inc(s, 2)
            pe.wait_ge(const_in, 80)

            def tile(t, k):
                return t[:, k * P:(k + 1) * P]

            def h0_transpose(g):
                pe.wait_ge(score_made, g + 1)
                pe.wait_ge(h0_made, g + 1)
                for k in range(GT):
                    last = nc.tensor.transpose(tile(PA, k), tile(H0, k), ident)
                last.then_inc(h0T_done, 1)

            def relation(g):
                pe.wait_ge(hT_made, g + 1)
                for k in range(GT):
                    last = nc.tensor.matmul(tile(PB, k), tile(HT, k), WREL[:, :], start=True, stop=True)
                last.then_inc(u_done, 1)

            def convolve(g):
                pe.wait_ge(u_made, g + 1)
                pe.wait_ge(adj_in, (g + 1) * 32)
                for k in range(GT):
                    nc.tensor.matmul(tile(PA, k), tile(HT, k), WROOT[:, :], start=True, stop=False)
                    last = nc.tensor.matmul(tile(PA, k), tile(ADJ, k), tile(U, k), start=False, stop=True)
                last.then_inc(conv_done, 1)

            def xn_transpose(g):
                pe.wait_ge(xn_made, g + 1)
                for k in range(GT):
                    last = nc.tensor.transpose(tile(PB, k), tile(XN, k), ident)
                last.then_inc(xnT_done, 1)

            def score(g):
                pe.wait_ge(xnT_made, g + 1)
                for k in range(GT):
                    last = nc.tensor.matmul(PA[:, k * E:(k + 1) * E], tile(XNT, k), WG[:, :], start=True, stop=True)
                last.then_inc(score_done, 1)

            def rank(q):
                pe.wait_ge(score_made, (q + 1) * NG + 1)
                pe.wait_ge(mask_made, q + 1)
                nc.tensor.matmul(PA[:, 0:E * TQ], KH[:, H_TRI:H_TRI + P], MK[:, :], start=True, stop=True)
                nc.tensor.matmul(PB[:, 0:E * TQ], KH[:, H_ONE:H_ONE + P], MK[:, :], start=True, stop=True).then_inc(rank_done, 1)

            def rows_transpose(b, j, loaded):
                if j % LB == 0:
                    pe.wait_ge(xb_in[j // LB], loaded)
                pe.wait_ge(xT_made, b + 1)
                src = XB[:, j * P:(j + 1) * P].bitcast(F16)
                for s in range(2):
                    last = nc.tensor.transpose(PX[j % 2][:, s * P:(s + 1) * P], src[:, s * P:(s + 1) * P], ident16)
                last.then_inc(xT_done, 1)

            def hidden(b, j, e):
                pe.wait_ge(xT_made, b + 3)
                pe.wait_ge(lo_made, b + 1)
                ph = PH[j % 2]
                hi = XT[:, j % 2 * 2 * P:j % 2 * 2 * P + P]
                lo = XT[:, j % 2 * 2 * P + P:j % 2 * 2 * P + 2 * P]
                nc.tensor.matmul(ph[:, :], cols(B1, e, P), KH[:, H_B1M:H_B1M + HID], start=True, stop=False, skip_group_check=True)
                for c in range(C):
                    for w, v in ((W1H, hi), (W1H, lo), (W1L, hi)):
                        last = nc.tensor.matmul(tile(ph, c), cols(w, e * C + c * P, P), v, start=False,
                                                stop=(c == C - 1 and w is W1L), skip_group_check=True)
                last.then_inc(h_done, 1)

            def output(b, j, e):
                pe.wait_ge(lo_made, b + 3)
                pe.wait_ge(y_made, b + 1)
                py = PY[j % 2][:, 0:P]
                nc.tensor.matmul(py, KH[:, H_B2M:H_B2M + P], cols(B2, e, P), start=True, stop=False)
                for c in range(C):
                    at = j % 2 * HID + c * P
                    hi, lo = HH[:, at:at + P], HL[:, at:at + P]
                    for h, w in ((hi, W2H), (hi, W2L), (lo, W2H)):
                        last = nc.tensor.matmul(py, h, cols(w, e * C + c * P, P), start=False,
                                                stop=(c == C - 1 and h is lo))
                last.then_inc(y_done, 1)

            def expert(b):
                return pe.value_load(BEI[0:1, bass.ds(b, 1)], min_val=0, max_val=(E - 1) * P)

            for q in range(2):
                if q:
                    pe.wait_ge(rank_used, q)
                with pe.Fori(0, NG) as i:
                    g = q * NG + i
                    h0_transpose(g)
                    relation(g)
                    convolve(g)
                    xn_transpose(g)
                    score(g)
                rank(q)
            pe.wait_ge(wlo_made, 2)
            pe.wait_ge(bias_made, 4)
            rows_transpose(0, 0, 16)
            for q in range(Q):
                graph = q + 2 < Q
                pe.wait_ge(experts_made, q + 1)
                if graph:
                    pe.wait_ge(rank_used, q + 2)

                def blocks_pass(i, first=False, last=False):
                    g = (q + 2) * NG + i
                    pieces = {2: lambda: h0_transpose(g), 3: lambda: relation(g), 5: lambda: convolve(g),
                              8: lambda: xn_transpose(g), 9: lambda: score(g)} if graph else {}
                    for j in range(SB):
                        b = q * NB + i * SB + j
                        if j + 1 < SB:
                            rows_transpose(b + 1, j + 1, (q * NG + i + 1) * 16)
                        elif not last:
                            rows_transpose(b + 1, 0, (q * NG + i + 2) * 16)
                        hidden(b, j, expert(b))
                        if not (first and j == 0):
                            output(b - 1, (j - 1) % SB, expert(b - 1))
                        if j in pieces:
                            pieces[j]()
                n0, n1 = (1 if q == 0 else 0), NG - (q == Q - 1)
                if n0:
                    blocks_pass(0, first=True)
                with pe.Fori(n0, n1) as i:
                    blocks_pass(i)
                if n1 < NG:
                    blocks_pass(n1, last=True)
                if graph:
                    rank(q + 2)
            output(Q * NB - 1, SB - 1, expert(Q * NB - 1))


def kernel(**inputs):
    import numpy as np
    import concourse.bacc as bacc
    from concourse.bass_utils import run_bass_kernel_spmd

    def c(a):
        return np.ascontiguousarray(a)

    a = {k: np.asarray(v) for k, v in inputs.items()}
    f32, f16 = np.float32, np.float16
    k = np.arange(P)
    kf = c(np.concatenate([
        np.eye(P, dtype=f32), np.ones((P, P), f32),
        np.broadcast_to(np.tile(a["L0_gnn_b_rel"], GT), (P, GW)),
        np.broadcast_to(np.tile(a["L0_ffn_bg"], GT), (P, GT * E)),
        np.broadcast_to(np.arange(E, 0, -1, dtype=f32), (P, E)),
        np.broadcast_to(np.arange(NB, dtype=f32) * P, (P, NB)),
        a["L0_gnn_ln_gamma"][:, None], a["L0_gnn_ln_beta"][:, None]], axis=1))
    b1m = np.zeros((P, C, P), f16)
    b2m = np.zeros((P, P), f16)
    for n in range(C):
        b1m[n, n] = b1m[32 + n, n] = 1
    b2m[0] = b2m[32] = 64
    kh = c(np.concatenate([np.eye(P, dtype=f16), (k[:, None] < k[None, :]).astype(f16), np.ones((P, P), f16),
                           b1m.reshape(P, C * P), b2m], axis=1))
    arrays = {
        "x": c(a["x"].reshape(TILES, P, P).transpose(1, 0, 2).reshape(P, TILES * P)),
        "adj": c(a["adj"].reshape(TILES, 2, 64, 64).transpose(1, 3, 0, 2).reshape(P, TILES * 64)),
        "wrel": c(a["L0_gnn_W_rel"]), "wroot": c(a["L0_gnn_W_root"]), "wg": c(a["L0_ffn_Wg"].T),
        "w1": c(a["L0_ffn_W1"].transpose(2, 0, 1).reshape(P, E * HID)),
        "w2": c(a["L0_ffn_W2"].reshape(E, P, C, P).transpose(3, 0, 2, 1).reshape(P, E * HID)),
        "b1": c(a["L0_ffn_b1"].reshape(E, C, P).transpose(1, 0, 2).reshape(C, E * P)),
        "b2": c(a["L0_ffn_b2"].reshape(1, E * P)),
        "kf": kf, "kh": kh,
    }
    nc = bacc.Bacc("TRN2", target_bir_lowering=False, num_devices=1)
    aps = {n: nc.dram_tensor("in_" + n, v.shape, mybir.dt.from_np(v.dtype), kind="ExternalInput").ap()
           for n, v in arrays.items()}
    out = nc.dram_tensor("out", (P, TILES * P), F32, kind="ExternalOutput").ap()
    build(nc, **aps, out=out)
    r = run_bass_kernel_spmd(nc, [{"in_" + n: v for n, v in arrays.items()}], core_ids=[0])
    res = r.results[0]["out"]
    return np.ascontiguousarray(res.reshape(P, TILES, P).transpose(1, 0, 2).reshape(a["x"].shape))
```

```python
import concourse.bass as bass
import concourse.mybir as mybir
from contextlib import ExitStack

F32 = mybir.dt.float32
F16 = mybir.dt.float16
I32 = mybir.dt.int32
ACT = mybir.ActivationFunctionType
ALU = mybir.AluOpType
AXX = mybir.AxisListType.X

P = 128
E = 8
HID = 512
C = HID // P
TILES = 64
Q = 4
TQ = TILES // Q
GT = 4
NG = TQ // GT
BW = 2 * P
NB = TQ + E
NR = NB * 2
SB = NB // NG
LB = SB // 2
LW = LB * BW
GW = GT * P
EPS = 1e-5
XS = 4.0
W1S = 32.0
W2S = 64.0
HS = XS * W1S
YS = HS * W2S
NEG = -3.0e38

K_ID, K_ONE, K_BREL, K_BG, K_DESC, K_FIRST, K_GAM, K_BET, K_END = (
    0, 128, 256, 768, 800, 808, 832, 833, 834)
H_ID, H_TRI, H_ONE, H_B1M, H_B2M, H_END = 0, 128, 256, 384, 1408, 1536


def build(nc, x, adj, wrel, wroot, wg, w1, w2, b1, b2, kf, kh, out):
    ctx = ExitStack()
    with ctx:
        def sb(name, shape, dt=F32):
            return ctx.enter_context(nc.sbuf_tensor(name, shape, dt))

        def pb(name, dt=F32):
            return ctx.enter_context(nc.psum_tensor(name, [P, 512], dt))

        def sem(name):
            return ctx.enter_context(nc.semaphore(name))


        rows = [nc.dram_tensor(f"rows{q}", [P * NR, P], F32, kind="Internal").ap() for q in range(Q)]
        yrows = [nc.dram_tensor(f"yrows{q}", [P * NR, P], F32, kind="Internal").ap() for q in range(Q)]
        rows_p = [r.rearrange("(p b) d -> p (b d)", p=P) for r in rows]
        yrows_p = [r.rearrange("(p b) d -> p (b d)", p=P) for r in yrows]

        KF = sb("KF", [P, K_END])
        KH = sb("KH", [P, H_END], F16)
        WREL = sb("WREL", [P, P])
        WROOT = sb("WROOT", [P, P])
        WG = sb("WG", [P, E])
        X = sb("X", [P, TILES * P])
        ADJ = sb("ADJ", [P, NG * GW])
        YG = [sb("YG0", [P, 2 * TQ * P]), sb("YG1", [P, 2 * TQ * P])]
        W1H = sb("W1H", [P, E * HID], F16)
        W1L = sb("W1L", [P, E * HID], F16)
        W2H = sb("W2H", [P, E * HID], F16)
        W2L = sb("W2L", [P, E * HID], F16)
        B1 = sb("B1", [P, E * P], F16)
        B2 = sb("B2", [P, E * P], F16)
        N4 = sb("N4", [P, NG * GW])
        T4 = sb("T4", [P, NG * GW])
        U4 = sb("U4", [P, NG * GW])
        TMP = sb("TMP", [P, GW])
        SCI = sb("SCI", [P, Q * 2 * TQ])
        SHI = sb("SHI", [P, Q * 2 * TQ])
        SC1 = sb("SC1", [P, Q * TQ])
        SCO = sb("SCO", [P, TQ])
        SHO = sb("SHO", [P, TQ])
        ST = sb("ST", [P, TQ * 6])
        MEAN2, MDIF, VARN = sb("MEAN2", [P, TQ]), sb("MDIF", [P, TQ]), sb("VARN", [P, TQ])
        IDLE, IDLA = sb("IDLE", [P, 1]), sb("IDLA", [P, 1])
        RA = sb("RA", [P, 2 * TQ])
        RT = sb("RT", [P, 2 * TQ])
        XHL = sb("XHL", [P, 2 * TQ * 2 * P], F16)
        LG = sb("LG", [P, TQ * E])
        M1 = sb("M1", [P, TQ])
        M2 = sb("M2", [P, TQ])
        KM = sb("KM", [P, TQ])
        EQ = sb("EQ", [P, TQ * E])
        OH = sb("OH", [P, 2 * TQ * E])
        LG2 = sb("LG2", [P, TQ * E])
        DM = sb("DM", [P, TQ])
        EX = sb("EX", [P, TQ])
        DEN = sb("DEN", [P, TQ])
        PR = sb("PR", [P, Q * 2 * TQ])
        MK = sb("MK", [P, E * TQ], F16)
        TOT = sb("TOT", [P, E * TQ])
        SC = sb("SC", [P, E * TQ])
        POS = sb("POS", [P, E * TQ])
        CNT = sb("CNT", [P, E])
        CNI = sb("CNI", [P, E], I32)
        PADI = sb("PADI", [P, E], I32)
        PADF = sb("PADF", [P, E])
        PEND = sb("PEND", [P, E])
        SHF = sb("SHF", [P, E])
        SLF = sb("SLF", [P, 2 * TQ])
        SLI = sb("SLI", [P, 2 * TQ], I32)
        SLA = sb("SLA", [P, 2 * TQ], I32)
        SLB = sb("SLB", [P, 2 * TQ], I32)
        SLC = sb("SLC", [P, 2 * TQ], I32)
        IDX = sb("IDX", [P, Q * 2 * TQ], I32)
        BEF = sb("BEF", [1, NB * (E - 1)])
        BES = sb("BES", [1, NB])
        BEI = sb("BEI", [1, Q * NB], I32)
        XB = sb("XB", [P, 2 * LW])
        XT = sb("XT", [P, 2 * 2 * BW], F16)
        HH = sb("HH", [P, 2 * C * BW], F16)
        HL = sb("HL", [P, 2 * C * BW], F16)
        YB = sb("YB", [P, 2 * LW])
        B1F, B2F, BT = YB[:, 0:E * P], HL[:, :].bitcast(F32), HH[:, :]
        ZERO = XB[:, :]

        PH = [pb("PH0"), pb("PH1")]
        PX = pb("PX")
        PC = pb("PC")
        PY = [pb("PY0"), pb("PY1")]
        PA, PB = pb("PA"), pb("PB")
        BK, BL = [*PH, PX, PC], [PA, PB, *PY]

        const_in = sem("const_in")
        x_in = [sem(f"x_in{q}") for q in range(Q)]
        adj_zero, adj_in = sem("adj_zero"), [sem(f"adj_in{k}") for k in range(NG)]
        w1_in, w2_in, b_in = sem("w1_in"), sem("w2_in"), sem("b_in")
        zero_made = sem("zero_made")
        zero_out = [sem(f"zero_out{q}") for q in range(Q)]
        scaled, whi_made, wlo_made, bhi_made, bt_made, bias_made, bias_zero = (
            sem("scaled"), sem("whi_made"), sem("wlo_made"), sem("bhi_made"), sem("bt_made"), sem("bias_made"), sem("bias_zero"))
        dve_step = sem("dve_step")
        dve_own = [sem(f"dve_own{n}") for n in range(18)]
        dve_sum = sem("dve_sum")
        stats_made, sum_made = sem("stats_made"), sem("sum_made")
        h0_made, h0T_done, hT_made = sem("h0_made"), sem("h0T_done"), sem("hT_made")
        scale_made = sem("scale_made")
        u_done, u_made, conv_done = sem("u_done"), sem("u_made"), sem("conv_done")
        xn_made, xhi_made, xlo_made = sem("xn_made"), sem("xhi_made"), sem("xlo_made")
        xnT_done, xnT_made, score_done, score_made = (
            sem("xnT_done"), sem("xnT_made"), sem("score_done"), sem("score_made"))
        gap_made, ex_made, mask_made, rank_done = sem("gap_made"), sem("ex_made"), sem("mask_made"), sem("rank_done")
        rank_used, slots_made, experts_made = sem("rank_used"), sem("slots_made"), sem("experts_made")
        scattered = [sem(f"scattered{q}") for q in range(Q)]
        xb_in = [sem("xb_in0"), sem("xb_in1")]
        def per_block(name):
            return [sem(f"{name}{j}") for j in range(SB)]
        xT_done, xT_made = per_block("xT_done"), per_block("xT_made")
        ha_done, hb_done = per_block("ha_done"), per_block("hb_done")
        hia_made, hib_made = per_block("hia_made"), per_block("hib_made")
        loa_made, lob_made = per_block("loa_made"), per_block("lob_made")
        y_done, y_made = per_block("y_done"), per_block("y_made")
        y_out = [sem("y_out0"), sem("y_out1")]
        gathered = [[sem(f"gathered{q}_{i}") for i in range(NG)] for q in range(Q)]
        combined, out_done = sem("combined"), sem("out_done")

        block = ctx.enter_context(nc.Block())

        def cols(t, start, size):
            return t[:, bass.ds(start, size)]

        def value(eng, v):
            return v if isinstance(v, int) else eng.snap(v)

        def hi_lo(q, i):
            v = cols(XHL, (q % 2 * TQ + i * GT) * 2 * P, 2 * GW).rearrange("p (t s d) -> p s t d", s=2, d=P)
            return v[:, 0], v[:, 1]

        @block.sync
        def _(sp):
            sp.sem_inc(y_out[0], 16)
            sp.sem_inc(y_out[1], 16)
            sp.dma_start(X[:, 0:TQ * P], x[:, 0:TQ * P]).then_inc(x_in[0], 16)
            sp.dma_start(KF[:, :], kf[:, :]).then_inc(const_in, 16)
            sp.dma_start(KH[:, :], kh[:, :]).then_inc(const_in, 16)
            sp.dma_start(WREL[:, :], wrel[:, :]).then_inc(const_in, 16)
            sp.dma_start(WROOT[:, :], wroot[:, :]).then_inc(const_in, 16)
            sp.dma_start(WG[:, :], wg[:, :]).then_inc(const_in, 16)

            def load_adj(k, g):
                d = ADJ[:, k * GW:(k + 1) * GW].rearrange("p (t c) -> p t c", c=P)
                s = adj[:, bass.ds(g * (GT * 64), GT * 64)].rearrange("p (t c) -> p t c", c=64)
                sp.dma_start(d[0:64, :, 0:64], s[0:64]).then_inc(adj_in[k], 16)
                sp.dma_start(d[64:P, :, 64:P], s[64:P]).then_inc(adj_in[k], 16)

            sp.wait_ge(adj_zero, 1)
            for k in range(NG):
                load_adj(k, k)
            sp.dma_start(YG[1][:, :], w2[:, :]).then_inc(w2_in, 16)
            for q in range(2, Q):
                sp.dma_start(X[:, q * TQ * P:(q + 1) * TQ * P], x[:, q * TQ * P:(q + 1) * TQ * P]).then_inc(x_in[q], 16)
            for k in range(NG):
                sp.wait_ge(conv_done, k + 2)
                load_adj(k, NG + k)

            def load_rows(q, c, j):
                sp.dma_start(XB[:, j * LW:(j + 1) * LW], rows_p[q][:, bass.ds(c * LW, LW)]).then_inc(xb_in[j], 16)

            sp.wait_ge(scattered[0], 2 * TQ * 16)
            for q in range(Q):
                sp.wait_ge(zero_out[q], 16)
            for j in range(2):
                load_rows(0, j, j)
            for q in range(Q):
                def chunk_pair(i, last):
                    n = q * NG + i
                    if q + 2 < Q:
                        sp.wait_ge(conv_done, 2 * NG + n + 1)
                        load_adj(0, 2 * NG + n)
                    for j in range(2):
                        end = (j + 1) * LB - 1
                        if not (last and q == Q - 1):
                            sp.wait_ge(xT_done[end], n + 2)
                            if last:
                                if j == 0:
                                    sp.wait_ge(scattered[q + 1], 2 * TQ * 16)
                                load_rows(q + 1, j, j)
                            else:
                                load_rows(q, 2 * i + 2 + j, j)
                        sp.wait_ge(y_made[end], n + 2)
                        sp.dma_start(yrows_p[q][:, bass.ds((2 * i + j) * LW, LW)],
                                     YB[:, j * LW:(j + 1) * LW]).then_inc(y_out[j], 16)
                with sp.Fori(0, NG - 1) as i:
                    chunk_pair(i, False)
                chunk_pair(NG - 1, True)

            with sp.Fori(0, Q * NG) as g:
                sp.wait_ge(combined, g + 1)
                sp.dma_start(out[:, bass.ds(g * GW, GW)], cols(X, g * GW, GW)).then_inc(out_done, 16)
            sp.wait_ge(out_done, Q * NG * 16)

        @block.gpsimd
        def _(pool):
            nc.gpsimd.memset(ADJ[:, :], 0.0).then_inc(adj_zero, 1)
            nc.gpsimd.memset(ZERO, 0.0).then_inc(zero_made, 1)
            nc.gpsimd.memset(B1[:, :], 0.0).then_inc(bias_zero, 1)
            nc.gpsimd.memset(B2[:, :], 0.0).then_inc(bias_zero, 1)
            for n, (w, s) in enumerate(((YG[0], W1S), (YG[1], W2S))):
                pool.wait_ge((w1_in, w2_in)[n], 16)
                nc.gpsimd.tensor_scalar(w[:, :], w[:, :], s, 1.0, ALU.mult, ALU.mult).then_inc(scaled, 1)
            for n, (w, hi, lo) in enumerate(((YG[0], W1H, W1L), (YG[1], W2H, W2L))):
                pool.wait_ge(whi_made, n + 1)
                nc.gpsimd.tensor_tensor(lo[:, :], w[:, :], hi[:, :], ALU.subtract).then_inc(wlo_made, 1)

            def scatter(q):
                pool.wait_ge(slots_made, q + 1)
                pool.wait_ge(xlo_made, (q + 1) * NG)
                pool.wait_ge(zero_out[q], 16)
                for t in range(TQ):
                    for k in range(2):
                        col = (q * 2 + k) * TQ + t
                        src = (q % 2 * TQ + t) * 2 * P
                        nc.gpsimd.indirect_dma_start(
                            rows[q], bass.IndirectOffsetOnAxis(ap=IDX[:, col:col + 1], axis=0),
                            XHL[:, src:src + 2 * P].bitcast(F32), None).then_inc(scattered[q], 16)

            def gather(q):
                for j in range(2):
                    pool.wait_ge(y_out[j], 16 + (q + 1) * 16 * NG)
                if q >= 2:
                    pool.wait_ge(combined, (q - 1) * NG)
                for t in range(TQ):
                    for k in range(2):
                        col = (q * 2 + k) * TQ + t
                        dst = (t * 2 + k) * P
                        nc.gpsimd.indirect_dma_start(
                            YG[q % 2][:, dst:dst + P], None, yrows[q],
                            bass.IndirectOffsetOnAxis(ap=IDX[:, col:col + 1], axis=0)).then_inc(gathered[q][t // GT], 16)

            scatter(0)
            scatter(1)
            scatter(2)
            gather(0)
            scatter(3)
            gather(1)
            gather(2)
            gather(3)
            for q in range(Q):
                for i in range(NG):
                    pool.wait_ge(gathered[q][i], 2 * GT * 16)

        @block.vector
        def _(dve):
            steps = [0]
            turn = [0, None]

            def step(ins):
                ins.then_inc(dve_step, 1)
                steps[0] += 1

            def settle():
                dve.wait_ge(dve_step, steps[0])

            def once(ins):
                step(ins)
                settle()

            def own(ins):
                ins.then_inc(dve_own[turn[0]], 1)
                dve.wait_ge(dve_own[turn[0]], turn[1])
                turn[0] += 1

            def guess(done, a, r, t):
                done(nc.vector.tensor_scalar(t.bitcast(I32), a.bitcast(I32), 1, None, ALU.logical_shift_right))
                done(nc.vector.tensor_scalar(r.bitcast(I32), t.bitcast(I32), -1.0, float(0x5F3759DF), ALU.mult, ALU.add))

            def newton(done, a, r, t):
                done(nc.vector.tensor_tensor(t, r, r, ALU.mult))
                done(nc.vector.scalar_tensor_tensor(t, t, -0.5, a, ALU.mult, ALU.mult))
                done(nc.vector.scalar_tensor_tensor(r, t, 1.5, r, ALU.add, ALU.mult))

            def rsqrt(done, a, r, t):
                guess(done, a, r, t)
                for _ in range(3):
                    newton(done, a, r, t)

            def moments(done, n):
                half = ST[:, 0:6 * n].rearrange("p (k s) -> p s k", s=6)
                nc.vector.tensor_tensor(MEAN2[:, 0:n], half[:, 1], half[:, 4], ALU.add)
                nc.vector.tensor_tensor(VARN[:, 0:n], half[:, 2], half[:, 5], ALU.add)
                done(nc.vector.tensor_tensor(MDIF[:, 0:n], half[:, 1], half[:, 4], ALU.subtract))
                done(nc.vector.tensor_tensor(MDIF[:, 0:n], MDIF[:, 0:n], MDIF[:, 0:n], ALU.mult))
                done(nc.vector.scalar_tensor_tensor(VARN[:, 0:n], MDIF[:, 0:n], P / 4.0, VARN[:, 0:n], ALU.mult, ALU.add))

            def scales_in(q):
                dve.wait_ge(x_in[q], 16)
                for t in range(TQ):
                    ins = nc.vector.bn_stats(ST[:, 6 * t:6 * t + 6], X[:, (q * TQ + t) * P:(q * TQ + t + 1) * P])
                once(ins)
                moments(once, TQ)
                nc.vector.tensor_scalar(RA[:, 0:TQ], VARN[:, :], 1.0 / P, EPS, ALU.mult, ALU.add)
                once(nc.vector.tensor_scalar(RA[:, TQ:2 * TQ], VARN[:, :], (1.0 + EPS) / P, EPS * EPS, ALU.mult, ALU.add))
                at = q * 2 * TQ
                rsqrt(once, RA[:, :], SCI[:, at:at + 2 * TQ], RT[:, :])
                nc.vector.tensor_scalar(SC1[:, q * TQ:(q + 1) * TQ], SCI[:, at:at + TQ], 1.0, None, ALU.add)
                for n in range(2):
                    ins = nc.vector.scalar_tensor_tensor(SHI[:, at + n * TQ:at + (n + 1) * TQ], MEAN2[:, :], -0.5,
                                                         SCI[:, at + n * TQ:at + (n + 1) * TQ], ALU.mult, ALU.mult)
                ins.then_inc(stats_made, 1)
                dve.wait_ge(stats_made, q + 1)

            def norm_in(q, k):
                for t in range(GT * k, GT * k + GT):
                    at = (q * 2 + 1) * TQ + t
                    ins = nc.vector.tensor_scalar(N4[:, t * P:(t + 1) * P], X[:, (q * TQ + t) * P:(q * TQ + t + 1) * P],
                                                  SCI[:, at:at + 1], SHI[:, at:at + 1], ALU.mult, ALU.add)
                ins.then_inc(h0_made, 1)

            def plus_norm(q, i):
                for k in range(GT):
                    xv = cols(X, (q * NG + i) * GW + k * P, P)
                    ins = nc.vector.tensor_scalar(xv, xv, cols(SC1, q * TQ + i * GT + k, 1),
                                                  cols(SHI, q * 2 * TQ + i * GT + k, 1), ALU.mult, ALU.add)
                ins.then_inc(sum_made, 1)

            def residual(done, q, i, bank, ready, summed):
                dve.wait_ge(conv_done, ready)
                done(nc.vector.tensor_tensor(TMP[:, :], bank[:, :], KF[:, K_BREL:K_BREL + GW], ALU.add))
                dve.wait_ge(sum_made, summed)
                xv = cols(X, (q * NG + i) * GW, GW)
                done(nc.vector.scalar_tensor_tensor(xv, TMP[:, :], 0.0, xv, ALU.max, ALU.add))

            def stats_out(done, q, i, at):
                nc.vector.memset(IDLE[:, :], 0.0)
                for k in range(GT):
                    ins = nc.vector.bn_stats(ST[:, 6 * (at + k):6 * (at + k) + 6], cols(X, (q * NG + i) * GW + k * P, P))
                done(ins)

            def variance_out(done, n):
                done(nc.vector.tensor_scalar(RA[:, 0:n], VARN[:, 0:n], 1.0 / P, EPS, ALU.mult, ALU.add))

            def shift_out(n):
                return nc.vector.scalar_tensor_tensor(SHO[:, 0:n], MEAN2[:, 0:n], -0.5, SCO[:, 0:n], ALU.mult, ALU.mult)

            def scales_out(done, n):
                variance_out(done, n)
                rsqrt(done, RA[:, 0:n], SCO[:, 0:n], RT[:, 0:n])
                done(shift_out(n))

            def norm_out(q, i, at):
                for k in range(at, at + GT):
                    ins = nc.vector.tensor_scalar(N4[:, k * P:(k + 1) * P], cols(X, (q * NG + i) * GW + (k - at) * P, P),
                                                  SCO[:, k:k + 1], SHO[:, k:k + 1], ALU.mult, ALU.add)
                ins.then_inc(xn_made, 1)

            def split_low(q, i, at, ready):
                dve.wait_ge(xhi_made, ready)
                hi, lo = hi_lo(q, i)
                nc.vector.scalar_tensor_tensor(lo, N4[:, at * P:at * P + GW].rearrange("p (t d) -> p t d", d=P), XS, hi,
                                               ALU.mult, ALU.subtract).then_inc(xlo_made, 1)

            def scores(i, bank, there):
                dve.wait_ge(score_done, there)
                nc.vector.tensor_tensor(cols(LG, i * (GT * E), GT * E), bank[:, 0:GT * E], KF[:, K_BG:K_BG + GT * E],
                                        ALU.add).then_inc(score_made, 1)

            def te(ap):
                return ap.rearrange("p (t e) -> p t e", e=E)

            def per_tile(t):
                return t[:, :].unsqueeze(2).to_broadcast([P, TQ, E])

            ohs = [OH[:, k * TQ * E:(k + 1) * TQ * E] for k in range(2)]

            def one_hot(src, m, k):
                desc = KF[:, K_DESC:K_DESC + E].unsqueeze(1).to_broadcast([P, TQ, E])
                step(nc.vector.tensor_reduce(m[:, :], te(src[:, :]), AXX, ALU.max)); settle()
                step(nc.vector.tensor_tensor(te(EQ[:, :]), te(src[:, :]), per_tile(m), ALU.is_equal)); settle()
                step(nc.vector.tensor_tensor(te(EQ[:, :]), te(EQ[:, :]), desc, ALU.mult)); settle()
                step(nc.vector.tensor_reduce(KM[:, :], te(EQ[:, :]), AXX, ALU.max)); settle()
                step(nc.vector.tensor_tensor(te(ohs[k]), te(EQ[:, :]), per_tile(KM), ALU.is_equal)); settle()

            def route_first(q):
                dve.wait_ge(score_made, (q + 1) * NG + 1)
                one_hot(LG, M1, 0)

            def route_second(q):
                step(nc.vector.scalar_tensor_tensor(LG2[:, :], ohs[0], NEG, LG[:, :], ALU.mult, ALU.add)); settle()
                one_hot(LG2, M2, 1)
                nc.vector.tensor_tensor(MK[:, :].rearrange("p (e t) -> p t e", t=TQ), te(ohs[0]), te(ohs[1]),
                                        ALU.add).then_inc(mask_made, 1)
                nc.vector.tensor_tensor(DM[:, :], M2[:, :], M1[:, :], ALU.subtract).then_inc(gap_made, 1)

            def et(t):
                return t[:, :].rearrange("p (e t) -> p e t", t=TQ)

            def route_slots(q):
                dve.wait_ge(rank_done, q + 1)
                step(nc.vector.tensor_copy(TOT[:, :], PC[:, E * TQ:2 * E * TQ])); settle()
                step(nc.vector.tensor_tensor_scan(SC[:, :], KF[:, K_ONE:K_ONE + E * TQ], TOT[:, :], 0.0, ALU.mult, ALU.add))
                step(nc.vector.tensor_reduce(CNT[:, :], et(TOT), AXX, ALU.add)); settle()
                step(nc.vector.tensor_tensor(POS[:, :], SC[:, :], TOT[:, :], ALU.subtract))
                step(nc.vector.tensor_scalar(CNI[:, :], CNT[:, :], float(BW - 1), None, ALU.add)); settle()
                step(nc.vector.tensor_tensor(POS[:, :], POS[:, :], PC[:, 0:E * TQ], ALU.add))
                step(nc.vector.tensor_scalar(PADI[:, :], CNI[:, :], 8, 8, ALU.logical_shift_right, ALU.logical_shift_left)); settle()
                step(nc.vector.tensor_copy(PADF[:, :], PADI[:, :])); settle()
                step(nc.vector.tensor_tensor_scan(PEND[:, :], KF[:, K_ONE:K_ONE + E], PADF[:, :], 0.0, ALU.mult, ALU.add)); settle()
                step(nc.vector.tensor_tensor(SHF[:, :], PEND[:, :], PADF[:, :], ALU.subtract)); settle()
                step(nc.vector.tensor_tensor(SHF[:, :], SHF[:, :], CNT[:, :], ALU.add)); settle()
                step(nc.vector.tensor_tensor(SHF[:, :], SHF[:, :], et(SC)[:, :, TQ - 1], ALU.subtract)); settle()
                nc.vector.tensor_tensor(et(POS), et(POS), SHF[:, :].unsqueeze(2).to_broadcast([P, E, TQ]), ALU.add).then_inc(rank_used, 1)

            def route_rows(q):
                dve.wait_ge(rank_used, q + 1)
                for k in range(2):
                    step(nc.vector.tensor_tensor(te(EQ[:, :]), te(ohs[k]), POS[:, :].rearrange("p (e t) -> p t e", t=TQ), ALU.mult)); settle()
                    step(nc.vector.tensor_reduce(SLF[:, k * TQ:(k + 1) * TQ], te(EQ[:, :]), AXX, ALU.add)); settle()
                step(nc.vector.tensor_copy(SLI[:, :], SLF[:, :])); settle()
                step(nc.vector.tensor_scalar(SLA[:, :], SLI[:, :], P - 1, None, ALU.bitwise_and))
                step(nc.vector.tensor_scalar(SLB[:, :], SLI[:, :], 7, None, ALU.logical_shift_right)); settle()
                nc.vector.scalar_tensor_tensor(IDX[:, q * 2 * TQ:(q + 1) * 2 * TQ], SLA[:, :], float(NR), SLB[:, :],
                                               ALU.mult, ALU.add).then_inc(slots_made, 1)

            def route_blocks(q):
                step(nc.vector.tensor_tensor(BEF[:, :].rearrange("p (b e) -> p b e", e=E - 1),
                                             KF[0:1, K_FIRST:K_FIRST + NB].unsqueeze(2).to_broadcast([1, NB, E - 1]),
                                             PEND[0:1, 0:E - 1].unsqueeze(1).to_broadcast([1, NB, E - 1]), ALU.is_ge)); settle()
                step(nc.vector.tensor_reduce(BES[:, :], BEF[:, :].rearrange("p (b e) -> p b e", e=E - 1), AXX, ALU.add)); settle()
                nc.vector.tensor_scalar(BEI[:, q * NB:(q + 1) * NB], BES[:, :], float(P), None, ALU.mult).then_inc(experts_made, 1)
                p1 = PR[:, q * 2 * TQ:q * 2 * TQ + TQ]
                dve.wait_ge(ex_made, q + 1)
                step(nc.vector.tensor_scalar(DEN[:, :], EX[:, :], 1.0, None, ALU.add)); settle()
                step(nc.vector.reciprocal(p1, DEN[:, :])); settle()
                step(nc.vector.tensor_tensor(PR[:, q * 2 * TQ + TQ:(q + 1) * 2 * TQ], EX[:, :], p1, ALU.mult)); settle()

            def xT_copy(j, ready, free):
                dve.wait_ge(xT_done[j], ready)
                dve.wait_ge(hb_done[j - 2], free)
                nc.vector.tensor_copy(XT[:, j % 2 * 2 * BW:(j % 2 + 1) * 2 * BW], PX[:, 0:BW].bitcast(F16)).then_inc(xT_made[j], 1)

            def low_half(j, h, ready):
                dve.wait_ge((hia_made, hib_made)[h][j], ready)
                at = (j % 2 * 2 + h) * 2 * BW
                nc.vector.scalar_tensor_tensor(HL[:, at:at + 2 * BW], PH[h][:, :], 0.0, HH[:, at:at + 2 * BW],
                                               ALU.max, ALU.subtract).then_inc((loa_made, lob_made)[h][j], 1)

            def combine(q, i, e):
                if e:
                    dve.wait_ge(dve_sum, q * NG + i + 1)
                for k in range(GT):
                    xv = cols(X, (q * NG + i) * GW + k * P, P)
                    y = cols(YG[q % 2], (i * GT + k) * 2 * P + e * P, P)
                    ins = nc.vector.scalar_tensor_tensor(xv, y, cols(PR, (q * 2 + e) * TQ + i * GT + k, 1), xv, ALU.mult, ALU.add)
                ins.then_inc(combined if e else dve_sum, 1)

            for s in (*xT_made, *loa_made, *lob_made, score_made):
                dve.sem_inc(s, 1)
            dve.wait_ge(const_in, 80)

            def biases_low():
                dve.wait_ge(bt_made, 2)
                for dst, src, r, s, v in ((B1, B1F, 4, HS, BT[:, 0:E * P]), (B2, B2F, 1, YS / 64.0, BT[:, E * P:2 * E * P])):
                    nc.vector.scalar_tensor_tensor(dst[32:32 + r, :], src[32:32 + r, :], s, v[32:32 + r, :],
                                                   ALU.mult, ALU.subtract).then_inc(bias_made, 1)

            def graph_quarter(q):
                for k in range(NG):
                    if q:
                        dve.wait_ge(xnT_done, (q - 1) * NG + k + 2)
                        dve.wait_ge(xhi_made, (q - 1) * NG + k + 2)
                    norm_in(q, k)
                for k in range(NG):
                    plus_norm(q, k)
                scales_in(2 * q + 1)
                for k in range(NG):
                    residual(once, q, k, BK[k], q * NG + k + 2, q * NG + k + 1)
                    stats_out(once, q, k, k * GT)
                moments(once, TQ)
                scales_out(once, TQ)
                for k in range(NG):
                    norm_out(q, k, k * GT)
                for k in range(NG):
                    split_low(q, k, k * GT, q * NG + k + 2)
                if q == 0:
                    scales_in(2)
                else:
                    biases_low()
                for k in range(NG):
                    scores(k, BK[k], q * NG + k + 1)

            scales_in(0)
            for q in range(2):
                graph_quarter(q)
                for part in (route_first, route_second, route_slots, route_rows, route_blocks):
                    part(q)

            xT_copy(0, 2, 1)
            for q in range(Q):
                graph = q + 2 < Q
                if not graph:
                    for i in range(NG):
                        dve.wait_ge(gathered[q - 2][i], 2 * GT * 16)

                def blocks_pass(i, last=False):
                    n = q * NG + i
                    g = 2 * NG + n
                    free, ready, nxt = value(dve, n + 1), value(dve, n + 2), value(dve, n + 3)
                    early, pieces = [[] for _ in range(SB)], [[] for _ in range(SB)]
                    if graph:
                        gfree, gready = value(dve, g + 1), value(dve, g + 2)
                        turn[:] = 0, value(dve, n + 1)

                        root = RA[:, 0:GT], SCO[:, 0:GT], RT[:, 0:GT]
                        early[2] += [lambda: residual(own, q + 2, i, PA, gready, gfree)]
                        pieces[2] += [lambda: stats_out(own, q + 2, i, 0)]
                        early[3] += [lambda: moments(own, GT), lambda: variance_out(own, GT)]
                        pieces[3] += [lambda: guess(own, *root), lambda: newton(own, *root)]
                        early[4] += [lambda: newton(own, *root), lambda: newton(own, *root),
                                     lambda: shift_out(GT).then_inc(scale_made, 1)]
                        pieces[5] += [lambda: split_low(q + 2, i, 0, gready), lambda: scores(i, PA, gfree)]
                    else:
                        pieces[1] += [lambda: combine(q - 2, i, 0)]
                        pieces[3] += [lambda: combine(q - 2, i, 1)]
                    if isinstance(i, int) and i == 0 and 0 < q < Q - 1:
                        pieces[0].insert(0, lambda: route_first(q + 1))
                        pieces[1].insert(0, lambda: route_second(q + 1))
                        pieces[2] += [lambda: route_slots(q + 1), lambda: route_rows(q + 1)]
                        pieces[4] += [lambda: route_blocks(q + 1)]
                    for j in range(SB):
                        if j + 1 < SB:
                            xT_copy(j + 1, ready, ready if j + 1 >= 2 else free)
                        elif not last:
                            xT_copy(0, nxt, ready)
                        for piece in early[j]:
                            piece()
                        low_half(j, 0, ready)
                        low_half(j, 1, ready)
                        for piece in pieces[j]:
                            piece()
                blocks_pass(0)
                n1 = NG - (q == Q - 1)
                with dve.Fori(1, n1) as i:
                    blocks_pass(i)
                if n1 < NG:
                    blocks_pass(n1, True)
            for q in range(Q - 2, Q):
                for i in range(NG):
                    dve.wait_ge(gathered[q][i], 2 * GT * 16)
                    combine(q, i, 0)
                    combine(q, i, 1)

        @block.scalar
        def _(act):
            for s in (*hia_made, *hib_made, *y_made, xhi_made):
                act.sem_inc(s, 1)
            act.wait_ge(zero_made, 1)

            act.dma_start(YG[0][:, :], w1[:, :]).then_inc(w1_in, 16)
            act.dma_start(X[:, TQ * P:2 * TQ * P], x[:, TQ * P:2 * TQ * P]).then_inc(x_in[1], 16)
            for r in (0, 32):
                act.dma_start(B1F[r:r + 4, :], b1[:, :]).then_inc(b_in, 16)
                act.dma_start(B2F[r:r + 1, :], b2[:, :]).then_inc(b_in, 16)
            for q in range(Q):
                n = NR * P // (2 * LW)
                act.dma_start(rows_p[q].rearrange("p (n c) -> p n c", n=n),
                              ZERO.unsqueeze(1).to_broadcast([P, n, 2 * LW])).then_inc(zero_out[q], 16)

            def h0_make(q, i, free):
                act.wait_ge(xnT_done, free)
                act.wait_ge(xlo_made, value(act, free - 1))
                for k in range(GT):
                    ins = nc.scalar.activation(N4[:, k * P:(k + 1) * P], cols(X, (q * NG + i) * GW + k * P, P), ACT.Identity,
                                               bias=cols(SHI, (q * 2 + 1) * TQ + i * GT + k, 1),
                                               scale=cols(SCI, (q * 2 + 1) * TQ + i * GT + k, 1))
                ins.then_inc(h0_made, 1)

            def plus_norm_between(q, i):
                for k in range(GT):
                    xv = cols(X, (q * NG + i) * GW + k * P, P)
                    ins = nc.scalar.activation(xv, xv, ACT.Identity, bias=cols(SHI, q * 2 * TQ + i * GT + k, 1),
                                               scale=cols(SC1, q * TQ + i * GT + k, 1))
                ins.then_inc(sum_made, 1)

            def norm_out_between(q, i, there):
                act.wait_ge(scale_made, there)
                nc.scalar.copy(IDLA[:, :], SCO[:, 0:1])
                for k in range(GT):
                    ins = nc.scalar.activation(N4[:, k * P:(k + 1) * P], cols(X, (q * NG + i) * GW + k * P, P), ACT.Identity,
                                               bias=SHO[:, k:k + 1], scale=SCO[:, k:k + 1])
                ins.then_inc(xn_made, 1)

            def hT_copy(k, bank, ready):
                act.wait_ge(h0T_done, ready)
                nc.scalar.activation(T4[:, k * GW:(k + 1) * GW], bank[:, :], ACT.Identity, bias=KF[:, K_BET:K_BET + 1],
                                     scale=KF[:, K_GAM:K_GAM + 1]).then_inc(hT_made, 1)

            def u_copy(k, bank, there):
                act.wait_ge(u_done, there)
                nc.scalar.copy(U4[:, k * GW:(k + 1) * GW], bank[:, :]).then_inc(u_made, 1)

            def split_high(q, i, k, there):
                act.wait_ge(xn_made, there)
                nc.scalar.activation(hi_lo(q, i)[0], N4[:, k * GW:(k + 1) * GW].rearrange("p (t d) -> p t d", d=P), ACT.Copy,
                                     scale=XS).then_inc(xhi_made, 1)

            def xnT_copy(k, bank, ready):
                act.wait_ge(xnT_done, ready)
                nc.scalar.copy(T4[:, k * GW:(k + 1) * GW], bank[:, :]).then_inc(xnT_made, 1)

            def exp_gap(q):
                act.wait_ge(gap_made, q + 1)
                nc.scalar.activation(EX[:, :], DM[:, :], ACT.Exp).then_inc(ex_made, 1)

            def high_half(j, h, ready, free):
                act.wait_ge((ha_done, hb_done)[h][j], ready)
                if h == 0:
                    act.wait_ge(y_done[j - 2], free)
                at = (j % 2 * 2 + h) * 2 * BW
                nc.scalar.activation(HH[:, at:at + 2 * BW], PH[h][:, :], ACT.Relu).then_inc((hia_made, hib_made)[h][j], 1)

            def y_copy(j, ready, stored):
                act.wait_ge(y_done[j], ready)
                if j % LB == 0:
                    act.wait_ge(y_out[j // LB], stored)
                nc.scalar.mul(YB[:, j * BW:(j + 1) * BW], PY[j % 2][:, 0:BW], 1.0 / YS).then_inc(y_made[j], 1)

            act.wait_ge(const_in, 80)
            for q in range(2):
                for k in range(NG):
                    hT_copy(k, BK[k], q * NG + k + 2)
                for k in range(NG):
                    u_copy(k, BL[k], q * NG + k + 1)
                if q == 0:
                    for n, (w, hi) in enumerate(((YG[0], W1H), (YG[1], W2H))):
                        act.wait_ge(scaled, n + 1)
                        nc.scalar.copy(hi[:, :], w[:, :]).then_inc(whi_made, 1)
                for k in range(NG):
                    split_high(q, k, k, q * NG + k + 1)
                for k in range(NG):
                    xnT_copy(k, BL[k], q * NG + k + 2)
                if q == 0:
                    act.wait_ge(bias_zero, 2)
                    act.wait_ge(b_in, 64)
                    for dst, src, r, s, v in ((B1, B1F, 4, HS, BT[:, 0:E * P]), (B2, B2F, 1, YS / 64.0, BT[:, E * P:2 * E * P])):
                        nc.scalar.activation(dst[0:r, :], src[0:r, :], ACT.Copy, scale=s).then_inc(bias_made, 1)
                        nc.scalar.activation(v[32:32 + r, :], src[32:32 + r, :], ACT.Copy, scale=s).then_inc(bt_made, 1)
                exp_gap(q)
            act.wait_ge(bias_made, 4)
            act.wait_ge(stats_made, Q)
            for q in range(Q):
                graph = q + 2 < Q
                if graph:
                    act.wait_ge(scattered[q], 2 * TQ * 16)

                def blocks_pass(i, first=False):
                    n = q * NG + i
                    free, ready, stored = value(act, n + 1), value(act, n + 2), value(act, n * 16 + 16)
                    between, pieces = [[] for _ in range(SB)], [[] for _ in range(SB)]
                    if graph:
                        g = 2 * NG + n
                        gfree, gready = value(act, g + 1), value(act, g + 2)
                        between[0] += [lambda: h0_make(q + 2, i, gfree)]
                        pieces[0] += [lambda: hT_copy(0, PA, gready)]
                        between[1] += [lambda: u_copy(0, PB, gfree)]
                        pieces[1] += [lambda: plus_norm_between(q + 2, i)]
                        pieces[4] += [lambda: norm_out_between(q + 2, i, free)]
                        between[5] += [lambda: xnT_copy(0, PB, gready)]
                        pieces[5] += [lambda: split_high(q + 2, i, 0, gfree)]
                    if isinstance(i, int) and i == 0 and 0 < q < Q - 1:
                        pieces[3] += [lambda: exp_gap(q + 1)]
                    for j in range(SB):
                        high_half(j, 0, ready, ready if j >= 2 else free)
                        high_half(j, 1, ready, None)
                        for piece in between[j]:
                            piece()
                        if j > 0:
                            y_copy(j - 1, ready, stored)
                        elif not first:
                            y_copy(SB - 1, free, None)
                        for piece in pieces[j]:
                            piece()
                blocks_pass(0, first=q == 0)
                with act.Fori(1, NG) as i:
                    blocks_pass(i)
            y_copy(SB - 1, Q * NG + 1, None)

        @block.tensor
        def _(pe):
            ident, ident16 = KF[:, K_ID:K_ID + P], KH[:, H_ID:H_ID + P]
            for s in (h0T_done, xnT_done, conv_done, *xT_done, *ha_done, *hb_done, *y_done):
                pe.sem_inc(s, 1)
            pe.wait_ge(const_in, 80)

            def tile(t, k):
                return t[:, k * P:(k + 1) * P]

            def h0_transpose(k, bank, there):
                pe.wait_ge(h0_made, there)
                for t in range(GT):
                    last = nc.tensor.transpose(tile(bank, t), tile(N4, k * GT + t), ident)
                last.then_inc(h0T_done, 1)

            def relation(k, bank, there):
                pe.wait_ge(hT_made, there)
                for t in range(GT):
                    last = nc.tensor.matmul(tile(bank, t), tile(T4, k * GT + t), WREL[:, :], start=True, stop=True)
                last.then_inc(u_done, 1)

            def convolve(k, bank, there, loaded):
                pe.wait_ge(u_made, there)
                pe.wait_ge(adj_in[k], loaded)
                for t in range(GT):
                    nc.tensor.matmul(tile(bank, t), tile(T4, k * GT + t), WROOT[:, :], start=True, stop=False)
                    last = nc.tensor.matmul(tile(bank, t), tile(ADJ, k * GT + t), tile(U4, k * GT + t), start=False, stop=True)
                last.then_inc(conv_done, 1)

            def xn_transpose(k, bank, there):
                pe.wait_ge(xn_made, there)
                for t in range(GT):
                    last = nc.tensor.transpose(tile(bank, t), tile(N4, k * GT + t), ident)
                last.then_inc(xnT_done, 1)

            def score(k, bank, there):
                pe.wait_ge(xnT_made, there)
                for t in range(GT):
                    last = nc.tensor.matmul(bank[:, t * E:(t + 1) * E], tile(T4, k * GT + t), WG[:, :], start=True, stop=True)
                last.then_inc(score_done, 1)

            def rank(q):
                if q > 1:
                    pe.wait_ge(rank_used, q)
                else:
                    pe.wait_ge(score_made, (q + 1) * NG + 1)
                pe.wait_ge(mask_made, q + 1)
                nc.tensor.matmul(PC[:, 0:E * TQ], KH[:, H_TRI:H_TRI + P], MK[:, :], start=True, stop=True)
                nc.tensor.matmul(PC[:, E * TQ:2 * E * TQ], KH[:, H_ONE:H_ONE + P], MK[:, :], start=True, stop=True).then_inc(rank_done, 1)

            def rows_transpose(j, loaded, free):
                if j % LB == 0:
                    pe.wait_ge(xb_in[j // LB], loaded)
                pe.wait_ge(xT_made[j - 1], free)
                px = PX[:, 0:BW].bitcast(F16)
                for t in range(2):
                    src = XB[:, j * BW + t * P:j * BW + (t + 1) * P].bitcast(F16)
                    for s in range(2):
                        last = nc.tensor.transpose(px[:, s * BW + t * P:s * BW + (t + 1) * P],
                                                   src[:, s * P:(s + 1) * P], ident16)
                last.then_inc(xT_done[j], 1)

            def hidden(j, e, ready, free):
                pe.wait_ge(xT_made[j], ready)
                at = j % 2 * 2 * BW
                hi, lo = XT[:, at:at + BW], XT[:, at + BW:at + 2 * BW]
                for h in range(2):
                    ph = PH[h]
                    pe.wait_ge((loa_made, lob_made)[h][j - 1], free)
                    nc.tensor.matmul(ph[:, :], cols(B1, e, P), KH[:, H_B1M + h * 2 * BW:H_B1M + (h + 1) * 2 * BW],
                                     start=True, stop=False, skip_group_check=True)
                    for c in (2 * h, 2 * h + 1):
                        for w, v in ((W1H, hi), (W1H, lo), (W1L, hi)):
                            last = nc.tensor.matmul(ph[:, c % 2 * BW:(c % 2 + 1) * BW], cols(w, e * C + c * P, P), v,
                                                    start=False, stop=(c % 2 == 1 and w is W1L), skip_group_check=True)
                    last.then_inc((ha_done, hb_done)[h][j], 1)

            def output(j, e, ready, free):
                pe.wait_ge(loa_made[j], ready)
                pe.wait_ge(lob_made[j], ready)
                pe.wait_ge(y_made[j - 2], free)
                py = PY[j % 2]
                nc.tensor.matmul(py[:, 0:BW], KH[:, H_B2M:H_B2M + P], cols(B2, e, P).unsqueeze(1).to_broadcast([P, 2, P]),
                                 start=True, stop=False, skip_group_check=True)
                for c in range(C):
                    for w in (W2H, W2L):
                        for t in range(2):
                            at = (j % 2 * C + c) * BW + t * P
                            for h in (HH, HL) if w is W2H else (HH,):
                                last = nc.tensor.matmul(py[:, t * P:(t + 1) * P], h[:, at:at + P], cols(w, e * C + c * P, P),
                                                        start=False, stop=(c == C - 1 and w is W2L), skip_group_check=True)
                last.then_inc(y_done[j], 1)

            def expert(b):
                return pe.value_load(BEI[0:1, bass.ds(b, 1)], min_val=0, max_val=(E - 1) * P)

            for q in range(2):
                for k in range(NG):
                    if q:
                        pe.wait_ge(score_made, (q - 1) * NG + k + 2)
                        if k == NG - 1:
                            pe.wait_ge(rank_used, q)
                    h0_transpose(k, BK[k], q * NG + k + 1)
                for k in range(NG):
                    relation(k, BL[k], q * NG + k + 1)
                for k in range(NG):
                    convolve(k, BK[k], q * NG + k + 1, (q + 1) * 32)
                for k in range(NG):
                    xn_transpose(k, BL[k], q * NG + k + 1)
                for k in range(NG):
                    score(k, BK[k], q * NG + k + 1)
                rank(q)
            pe.wait_ge(wlo_made, 2)
            pe.wait_ge(bias_made, 4)
            rows_transpose(0, 16, 1)
            for q in range(Q):
                graph = q + 2 < Q

                def blocks_pass(i, first=False, last=False):
                    n = q * NG + i
                    free, ready, loaded = value(pe, n + 1), value(pe, n + 2), value(pe, n * 16 + 16)
                    pieces, between = [[] for _ in range(SB)], [[] for _ in range(SB)]
                    if graph:
                        g = 2 * NG + n
                        gfree, adj_there = value(pe, g + 1), value(pe, n * 32 + 96)

                        def start_group():
                            pe.wait_ge(score_made, gfree)
                            h0_transpose(0, PA, gfree)
                        pieces[0] += [start_group]
                        between[1] += [lambda: relation(0, PB, gfree)]
                        pieces[1] += [lambda: convolve(0, PA, gfree, adj_there)]
                        between[5] += [lambda: xn_transpose(0, PB, gfree)]
                        pieces[5] += [lambda: score(0, PA, gfree)]
                    if isinstance(i, int) and i == 0 and 0 < q < Q - 1:
                        pieces[1] += [lambda: rank(q + 1)]
                    before = None if first else expert(n * SB - 1)
                    if isinstance(i, int) and i == 0:
                        pe.wait_ge(experts_made, q + 1)
                    for j in range(SB):
                        if j + 1 < SB:
                            rows_transpose(j + 1, loaded, ready if j + 1 >= 1 else free)
                        elif not last:
                            rows_transpose(0, value(pe, loaded + 16), ready)
                        e = expert(n * SB + j)
                        hidden(j, e, ready, ready if j else free)
                        for piece in between[j]:
                            piece()
                        if before is not None:
                            output((j - 1) % SB, before, ready if j else free, ready if j >= 3 else free)
                        before = e
                        for piece in pieces[j]:
                            piece()
                blocks_pass(0, first=q == 0)
                n1 = NG - (q == Q - 1)
                with pe.Fori(1, n1) as i:
                    blocks_pass(i)
                if n1 < NG:
                    blocks_pass(n1, last=True)
            output(SB - 1, expert(Q * NB - 1), Q * NG + 1, Q * NG + 1)


def kernel(**inputs):
    import numpy as np
    import concourse.bacc as bacc
    from concourse.bass_utils import run_bass_kernel_spmd

    def c(a):
        return np.ascontiguousarray(a)

    a = {k: np.asarray(v) for k, v in inputs.items()}
    f32, f16 = np.float32, np.float16
    k = np.arange(P)
    kf = c(np.concatenate([
        np.eye(P, dtype=f32), np.ones((P, P), f32),
        np.broadcast_to(np.tile(a["L0_gnn_b_rel"], GT), (P, GW)),
        np.broadcast_to(np.tile(a["L0_ffn_bg"], GT), (P, GT * E)),
        np.broadcast_to(np.arange(E, 0, -1, dtype=f32), (P, E)),
        np.broadcast_to(np.arange(NB, dtype=f32) * BW, (P, NB)),
        a["L0_gnn_ln_gamma"][:, None], a["L0_gnn_ln_beta"][:, None]], axis=1))
    b1m = np.zeros((P, C, BW), f16)
    b2m = np.zeros((P, P), f16)
    for n in range(C):
        b1m[n, n] = b1m[32 + n, n] = 1
    b2m[0] = b2m[32] = 64
    kh = c(np.concatenate([np.eye(P, dtype=f16), (k[:, None] < k[None, :]).astype(f16), np.ones((P, P), f16),
                           b1m.reshape(P, C * BW), b2m], axis=1))
    arrays = {
        "x": c(a["x"].reshape(TILES, P, P).transpose(1, 0, 2).reshape(P, TILES * P)),
        "adj": c(a["adj"].reshape(TILES, 2, 64, 64).transpose(1, 3, 0, 2).reshape(P, TILES * 64)),
        "wrel": c(a["L0_gnn_W_rel"]), "wroot": c(a["L0_gnn_W_root"]), "wg": c(a["L0_ffn_Wg"].T),
        "w1": c(a["L0_ffn_W1"].transpose(2, 0, 1).reshape(P, E * HID)),
        "w2": c(a["L0_ffn_W2"].reshape(E, P, C, P).transpose(3, 0, 2, 1).reshape(P, E * HID)),
        "b1": c(a["L0_ffn_b1"].reshape(E, C, P).transpose(1, 0, 2).reshape(C, E * P)),
        "b2": c(a["L0_ffn_b2"].reshape(1, E * P)),
        "kf": kf, "kh": kh,
    }
    nc = bacc.Bacc("TRN2", target_bir_lowering=False, num_devices=1)
    aps = {n: nc.dram_tensor("in_" + n, v.shape, mybir.dt.from_np(v.dtype), kind="ExternalInput").ap()
           for n, v in arrays.items()}
    out = nc.dram_tensor("out", (P, TILES * P), F32, kind="ExternalOutput").ap()
    build(nc, **aps, out=out)
    r = run_bass_kernel_spmd(nc, [{"in_" + n: v for n, v in arrays.items()}], core_ids=[0])
    res = r.results[0]["out"]
    return np.ascontiguousarray(res.reshape(P, TILES, P).transpose(1, 0, 2).reshape(a["x"].shape))
```
